# Optimizing a Trainium2 kernel written in Bass

```python
import numpy as np
import jax
import jax.numpy as jnp

def _softmax(x, axis=-1):
    return jax.nn.softmax(x, axis=axis)

def _gelu(x):
    return jax.nn.gelu(x, approximate=True)

def _silu(x):
    return jax.nn.silu(x)

def _sigmoid(x):
    return jax.nn.sigmoid(x)

def _layernorm(x, axis=-1, eps=1e-05):
    m = jnp.mean(x, axis=axis, keepdims=True)
    v = jnp.var(x, axis=axis, keepdims=True)
    return (x - m) / jnp.sqrt(v + eps)

def _scatter_add(tgt, idx, src, axis=0):
    return tgt.at[idx].add(src)

def _segment_sum(src, seg, n):
    return jax.ops.segment_sum(src, seg, n)
kernel_name = 'mk_macaron_d1_jaxref_r8_ec3ba4'

def setup_inputs(seed: int=0):
    np.random.seed(seed)
    _w = jnp.asarray

    def _L0_attn_setup():
        import jax, jax.numpy as jnp
        import numpy as np
        DIM = 128
        NUM_HEADS = 16
        HEAD_DIM = DIM // NUM_HEADS
        ROPE_BASE = 10000.0

        def rope_cos_sin(seq_len, dim):
            inv_freq = 1.0 / ROPE_BASE ** (jnp.arange(0, dim, 2, dtype=jnp.float32) / dim)
            t = jnp.arange(seq_len, dtype=jnp.float32)
            freqs = t[:, None] * inv_freq[None, :]
            emb = jnp.concatenate([freqs, freqs], axis=-1)
            return (jnp.cos(emb), jnp.sin(emb))

        def apply_rotary(x, cos, sin):
            x1 = x[..., ::2]
            x2 = x[..., 1::2]
            x_rot = jnp.stack((-x2, x1), axis=-1).reshape(x.shape)
            return x * cos + x_rot * sin
        key = jax.random.key(seed)
        ks = jax.random.split(key, 5)
        B, L, C = (4, 256, DIM)
        s = 1.0 / np.sqrt(C)
        return {'x': jax.random.normal(ks[0], (B, L, C), dtype=jnp.float32), 'qkv_w': jax.random.normal(ks[1], (3 * C, C), dtype=jnp.float32) * s, 'qkv_b': jax.random.normal(ks[2], (3 * C,), dtype=jnp.float32) * 0.02, 'proj_w': jax.random.normal(ks[3], (C, C), dtype=jnp.float32) * s, 'proj_b': jax.random.normal(ks[4], (C,), dtype=jnp.float32) * 0.02}
    _L0_attn_in = _L0_attn_setup()

    def _L0_ffn_setup():
        import jax, jax.numpy as jnp
        import numpy as np
        DIM = 128
        HIDDEN = 384
        SCALE = 1.0 / 127.0

        def _dequant(w_int, dtype):
            return w_int.astype(dtype) * jnp.asarray(SCALE, dtype)
        key = jax.random.key(seed)
        k_x, k_g, k_u, k_d = jax.random.split(key, 4)
        x = jax.random.normal(k_x, (4, 256, DIM), dtype=jnp.float32)
        w_gate = jax.random.randint(k_g, (HIDDEN, DIM), -127, 128, dtype=jnp.int32)
        w_up = jax.random.randint(k_u, (HIDDEN, DIM), -127, 128, dtype=jnp.int32)
        w_down = jax.random.randint(k_d, (DIM, HIDDEN), -127, 128, dtype=jnp.int32)
        return {'x': x, 'w_gate': w_gate, 'w_up': w_up, 'w_down': w_down}
    _L0_ffn_in = _L0_ffn_setup()
    _d = {'L0_attn_x': _L0_attn_in['x'], 'L0_attn_qkv_w': _L0_attn_in['qkv_w'], 'L0_attn_qkv_b': _L0_attn_in['qkv_b'], 'L0_attn_proj_w': _L0_attn_in['proj_w'], 'L0_attn_proj_b': _L0_attn_in['proj_b'], 'L0_ffn_w_gate': _L0_ffn_in['w_gate'], 'L0_ffn_w_up': _L0_ffn_in['w_up'], 'L0_ffn_w_down': _L0_ffn_in['w_down']}
    _x0 = _d['L0_attn_x']
    _d['L0_attn_x'] = jax.random.normal(jax.random.fold_in(jax.random.key(seed), 1), (16, 512, 128), dtype=_x0.dtype)
    del _x0
    return _d

def reference(L0_attn_x, L0_attn_qkv_w, L0_attn_qkv_b, L0_attn_proj_w, L0_attn_proj_b, L0_ffn_w_gate, L0_ffn_w_up, L0_ffn_w_down):

    def _L0_attn_ref(x, qkv_w, qkv_b, proj_w, proj_b):
        import jax, jax.numpy as jnp
        import numpy as np
        DIM = 128
        NUM_HEADS = 16
        HEAD_DIM = DIM // NUM_HEADS
        ROPE_BASE = 10000.0

        def rope_cos_sin(seq_len, dim):
            inv_freq = 1.0 / ROPE_BASE ** (jnp.arange(0, dim, 2, dtype=jnp.float32) / dim)
            t = jnp.arange(seq_len, dtype=jnp.float32)
            freqs = t[:, None] * inv_freq[None, :]
            emb = jnp.concatenate([freqs, freqs], axis=-1)
            return (jnp.cos(emb), jnp.sin(emb))

        def apply_rotary(x, cos, sin):
            x1 = x[..., ::2]
            x2 = x[..., 1::2]
            x_rot = jnp.stack((-x2, x1), axis=-1).reshape(x.shape)
            return x * cos + x_rot * sin
        B, L, C = x.shape
        H, D = (NUM_HEADS, HEAD_DIM)
        scale = D ** (-0.5)
        qkv = x @ qkv_w.T + qkv_b
        qkv = qkv.reshape(B, L, 3, H, D).transpose(2, 0, 3, 1, 4)
        q, k, v = (qkv[0], qkv[1], qkv[2])
        cos, sin = rope_cos_sin(L, D)
        q = apply_rotary(q, cos, sin)
        k = apply_rotary(k, cos, sin)
        attn = jnp.einsum('bhqd,bhkd->bhqk', q, k) * scale
        attn = jax.nn.softmax(attn, axis=-1)
        out = jnp.einsum('bhqk,bhkd->bhqd', attn, v)
        out = out.transpose(0, 2, 1, 3).reshape(B, L, C)
        return out @ proj_w.T + proj_b

    def _L0_ffn_ref(x, w_gate, w_up, w_down):
        import jax, jax.numpy as jnp
        import numpy as np
        DIM = 128
        HIDDEN = 384
        SCALE = 1.0 / 127.0

        def _dequant(w_int, dtype):
            return w_int.astype(dtype) * jnp.asarray(SCALE, dtype)
        wg = _dequant(w_gate, x.dtype)
        wu = _dequant(w_up, x.dtype)
        wd = _dequant(w_down, x.dtype)
        gate = jnp.einsum('bsd,hd->bsh', x, wg)
        up = jnp.einsum('bsd,hd->bsh', x, wu)
        h = jax.nn.silu(gate) * up
        return jnp.einsum('bsh,dh->bsd', h, wd)
    x = L0_attn_x
    x = x + 0.5 * _L0_ffn_ref(_layernorm(x, axis=-1), L0_ffn_w_gate, L0_ffn_w_up, L0_ffn_w_down)
    x = x + _L0_attn_ref(_layernorm(x, axis=-1), L0_attn_qkv_w, L0_attn_qkv_b, L0_attn_proj_w, L0_attn_proj_b)
    x = x + 0.5 * _L0_ffn_ref(_layernorm(x, axis=-1), L0_ffn_w_gate, L0_ffn_w_up, L0_ffn_w_down)
    return x

_drawn_inputs = setup_inputs


def setup_inputs(seed=0):
    import zlib

    import numpy as np

    out = dict(_drawn_inputs(seed))
    spreads = {}
    factors = {'L0_attn_qkv_w': 8.0, 'L0_attn_qkv_b': 8.0, 'L0_attn_proj_w': 8.0, 'L0_attn_proj_b': 200.0}
    for name, (base, spread) in spreads.items():
        noise = np.random.default_rng([zlib.crc32(name.encode()), seed]).standard_normal(out[name].shape)
        drawn = base * np.exp(spread * noise) if base else spread * noise
        out[name] = jnp.asarray(drawn.astype(out[name].dtype))
    for name, factor in factors.items():
        out[name] = (out[name] * factor).astype(out[name].dtype)
    return out
```

```python
from contextlib import ExitStack

import concourse.bass as bass
from concourse import mybir

F32 = mybir.dt.float32
F32R = mybir.dt.float32r
I32 = mybir.dt.int32
ALU = mybir.AluOpType
ACT = mybir.ActivationFunctionType
AX_X = mybir.AxisListType.X

P = 128
B, L, C = 16, 512, 128
H, D = 16, 8
T = L // P
HID = 384
J = HID // P
GROUPS = H // 4
STRIP = 32
ROWS_MAX = 3 * D
ROWS_EXP = ROWS_MAX + 2
TILES = 4 * T
SLOTS = B * GROUPS
EPS = 1e-5
W_SCALE = 1.0 / 127.0
Q_SCALE = float(D) ** -0.5
N_DENSE = 3

DENSE = [
    [(0, "stats1"), (2, "norm1"), (3, "xT1"), (4, "gate1_0"), (5, "up1_0"), (7, "gate1_1"), (8, "up1_1"),
     (11, "gate1_2"), (12, "up1_2")],
    [(0, "attnT"), (1, "proj"), (2, "stats3"), (2, "down1"), (3, "stats2"), (4, "norm3"), (5, "norm2"),
     (6, "xT2"), (7, "qkv_0"), (8, "qkv_1"), (9, "qkv_2"), (11, "qkv_3"), (12, "xT3"), (14, "rope")],
    [(1, "gate2_0"), (3, "up2_0"), (6, "gate2_1"), (9, "up2_1")],
    [(2, "gate2_2"), (5, "up2_2"), (8, "down2")],
]
AHEAD = ("stats1", "norm1", "xT1", "gate1", "up1", "down1", "stats2", "norm2", "xT2", "qkv", "rope")
PV_AT = (1, 4, 7, 10)
MAX_SPAN = 12


def steps(b):
    out = []
    for g in range(GROUPS):
        s = GROUPS * b + g
        here, nxt, prev = 0 <= b < B, 0 <= s + 1 < SLOTS, 0 <= s - 1 < SLOTS
        if nxt:
            out += [("kT", g), ("qT", g)]
        v = 0
        for i in range(TILES):
            if here:
                out.append(("exp", g, i))
            for at, what in DENSE[g]:
                ahead = what.split("_")[0] in AHEAD
                if at == i and (0 <= b + 1 < B if ahead else 0 <= b - 1 < B):
                    out.append((what,))
            while nxt and v < min(TILES, (i + 1) * TILES // MAX_SPAN):
                out.append(("max", g, v))
                v += 1
            if prev and i in PV_AT:
                out.append(("pv", g, PV_AT.index(i)))
            if prev and i == 11:
                out.append(("oCopy", g))
            if nxt and i == 12:
                out += [("vAug", g), ("negMax", g)]
            if prev and i == 13:
                out.append(("oT", g))
            if nxt and i == 14:
                out.append(("qmT", g))
    return out


DENSE_USERS = ("kT", "qT", "qmT", "oT", "xT1", "xT2", "xT3", "attnT", "proj", "down1", "down2",
               "qkv_0", "qkv_1", "qkv_2", "qkv_3") + tuple(
                   f"{k}{f}_{j}" for k in ("gate", "up") for f in (1, 2) for j in range(J))


def number_uses():
    use, gate, stat = {}, {}, {}
    for b in range(-1, B + 1):
        for st in steps(b):
            if st[0] in DENSE_USERS:
                use[st, b] = len(use)
            if st[0].startswith("gate"):
                gate[st, b] = len(gate)
            if st[0].startswith("stats"):
                stat[st, b] = len(stat)
    return use, gate, stat


class Batch:

    def __init__(self, first, turn=None):
        self.first, self.turn = first, turn

    def value(self, per_batch, plus):
        v = per_batch * self.first + plus
        return v if self.turn is None else self.turn * (2 * per_batch) + v

    def counted(self, table, key, per=1, plus=0):
        v = table[key, self.first]
        if self.turn is None:
            return v // per + plus
        grow = table[key, self.first + 2] - v
        assert grow % per == 0 and grow == table[key, self.first + 4] - table[key, self.first + 2]
        return self.turn * (grow // per) + (v // per + plus)


def macaron_layer(nc, x, qkv_w, qkv_b, proj_w, proj_b, w_gate, w_up, w_down, rope_cos, rope_sin, out):
    USE, GATE, STAT = number_uses()
    with ExitStack() as ctx:
        def sb(name, shape, dt=F32):
            return ctx.enter_context(nc.sbuf_tensor(name, shape, dt))

        def sem(name):
            return ctx.enter_context(nc.semaphore(name))

        ident = sb("ident", [P, P])
        cos_t = sb("cos_t", [P, T, D])
        sin_t = sb("sin_t", [P, T, D])
        rows_int = sb("rows_int", [P, 3 * HID], I32)
        rows_ffn = sb("rows_ffn", [P, 9, P])
        rows_qkv = sb("rows_qkv", [P, 4, P])
        w_gateT = sb("w_gateT", [P, HID])
        w_upT = sb("w_upT", [P, HID])
        w_downT = sb("w_downT", [P, J, C])
        w_qkvT = sb("w_qkvT", [P, 3 * C])
        w_projT = sb("w_projT", [P, C])
        b_qkv = sb("b_qkv", [P, 3 * C])
        b_proj = sb("b_proj", [P, C])
        minus_half = sb("minus_half", [P, T])
        x_in = [sb(f"x_in{k}", [P, T, C]) for k in range(2)]
        x_ffn1 = [sb(f"x_ffn1{k}", [P, T, C]) for k in range(2)]
        x_attn = sb("x_attn", [P, T, C])
        y_out = sb("y_out", [P, T, C])
        stats = [sb(f"stats{k}", [P, T, 6]) for k in range(3)]
        mean_var = [sb(f"mean_var{k}", [P, T, 2]) for k in range(3)]
        var_eps = [sb(f"var_eps{k}", [P, T]) for k in range(3)]
        rstd = [sb(f"rstd{k}", [P, T]) for k in range(3)]
        x_hat = [sb(f"x_hat{k}", [P, T, C]) for k in range(3)]
        x_hatT = [sb(f"x_hatT{k}", [P, L]) for k in range(3)]
        tanh = [sb(f"tanh{k}", [P, J, L]) for k in range(2)]
        silu = [sb(f"silu{k}", [P, L]) for k in range(2)]
        hid = sb("hid", [P, J, L])
        qkv = [sb(f"qkv{k}", [P, T, 3 * C]) for k in range(2)]
        rot_a = sb("rot_a", [P, T, 2 * C])
        rot_b = sb("rot_b", [P, T, 2 * C])
        q_parts = [sb(f"q_parts{k}", [P, T, H, STRIP]) for k in range(2)]
        k_parts = [sb(f"k_parts{k}", [P, T, H, STRIP]) for k in range(2)]
        qT = sb("qT", [P, L], F32R)
        kT = [sb(f"kT{k}", [P, L], F32R) for k in range(2)]
        qmT = [sb(f"qmT{k}", [P, L], F32R) for k in range(2)]
        v_aug = [sb(f"v_aug{k}", [P, T, 4, STRIP]) for k in range(2)]
        neg_max = [sb(f"neg_max{k}", [P, 4, T]) for k in range(2)]
        probs = [sb(f"probs{k}", [P, 4, T, L]) for k in range(2)]
        oT = sb("oT", [P, L])
        recip = [sb(f"recip{k}", [P, T, 4]) for k in range(2)]
        attn = [sb(f"attn{k}", [P, T, C]) for k in range(2)]
        attnT = sb("attnT", [P, L])
        max_ps = [ctx.enter_context(nc.psum_tensor(f"max_ps{k}", [P, L], F32)) for k in range(2)]
        exp_ps = [ctx.enter_context(nc.psum_tensor(f"exp_ps{k}", [P, L], F32)) for k in range(2)]
        pv_ps = ctx.enter_context(nc.psum_tensor("pv_ps", [P, L], F32))
        dense_ps = [ctx.enter_context(nc.psum_tensor(f"dense_ps{k}", [P, L], F32)) for k in range(N_DENSE)]

        weights_in = sem("weights_in")
        tables_in = sem("tables_in")
        ident_zero = sem("ident_zero")
        ident_ready = sem("ident_ready")
        parts_set = sem("parts_set")
        dequantized = sem("dequantized")
        setup_T = sem("setup_T")
        weights_ready = sem("weights_ready")
        x_loaded = [sem(f"x_loaded{k}") for k in range(2)]
        stored = sem("stored")
        dense_ready = sem("dense_ready")
        dense_read = [sem(f"dense_read{k}") for k in range(N_DENSE)]
        tanh_ready = sem("tanh_ready")
        stats_part = sem("stats_part")
        stats_ready = [sem(f"stats_ready{k}") for k in range(3)]
        var_ready = sem("var_ready")
        rstd_ready = [sem(f"rstd_ready{k}") for k in range(3)]
        hat_ready = [sem(f"hat_ready{k}") for k in range(3)]
        rope_part = sem("rope_part")
        parts_ready = sem("parts_ready")
        v_ready = sem("v_ready")
        maxscore_ready = sem("maxscore_ready")
        max_done = sem("max_done")
        negmax_hi = sem("negmax_hi")
        negmax_ready = sem("negmax_ready")
        expscore_ready = sem("expscore_ready")
        exp_done = sem("exp_done")
        pv_done = sem("pv_done")
        o_copied = sem("o_copied")
        recip_done = sem("recip_done")
        proj_part = sem("proj_part")
        passed = sem("passed")

        def wait(eng, s, value):
            if not (isinstance(value, int) and value <= 0):
                eng.wait_ge(s, value)

        def settle(eng):
            eng.sem_inc(passed, 1)

        def wait_dense(eng, st, b):
            wait(eng, dense_ready, b.counted(USE, st, plus=1))

        def bank(st, b):
            return USE[st, b.first] % N_DENSE

        def wait_read(eng, st, b):
            wait(eng, dense_read[bank(st, b)], b.counted(USE, st, per=N_DENSE, plus=1))

        def slot(b, g):
            return Batch(b.first + g // GROUPS, b.turn), g % GROUPS

        def head_strip(hs, rows=STRIP):
            return slice(STRIP * hs, STRIP * hs + rows)

        def tile(t):
            return slice(t * P, (t + 1) * P)

        def program(run, eng):
            for b in (-1, 0):
                for st in steps(b):
                    run(st, Batch(b))
            with eng.Fori(0, (B - 2) // 2) as turn:
                for b in (1, 2):
                    for st in steps(b):
                        run(st, Batch(b, turn))
            for b in (B - 1, B):
                for st in steps(b):
                    run(st, Batch(b))

        x_d = x.rearrange("b (p t) c -> b p t c", t=T)
        out_d = out.rearrange("b (p t) c -> b p t c", t=T)
        block = ctx.enter_context(nc.Block())

        @block.sync
        def _(sp):
            n_w = 0
            for dst, src in (
                (rows_int[:, 0:HID].rearrange("p (j c) -> p j c", j=J), w_gate.rearrange("(j p) c -> p j c", p=P)),
                (rows_int[:, HID:2 * HID].rearrange("p (j c) -> p j c", j=J), w_up.rearrange("(j p) c -> p j c", p=P)),
                (rows_int[:, 2 * HID:3 * HID], w_down),
                (rows_qkv[:, 0:3, :], qkv_w.rearrange("(j p) c -> p j c", p=P)),
                (rows_qkv[:, 3, :], proj_w),
            ):
                sp.dma_start(dst, src).then_inc(weights_in, 16)
            for b in range(2):
                sp.dma_start(x_in[b][:], x_d[b]).then_inc(x_loaded[b], 16)
            sp.dma_start(b_qkv[:], qkv_b.unsqueeze(0).broadcast_to([P, 3 * C])).then_inc(tables_in, 16)
            sp.dma_start(b_proj[:], proj_b.unsqueeze(0).broadcast_to([P, C])).then_inc(tables_in, 16)
            sp.dma_start(cos_t[:], rope_cos.rearrange("(p t) d -> p t d", t=T)).then_inc(tables_in, 16)
            sp.dma_start(sin_t[:], rope_sin.rearrange("(p t) d -> p t d", t=T)).then_inc(tables_in, 16)

            def load_and_store(b, load, store):
                k = (b.first + 1) % 2
                if load:
                    wait_read(sp, ("down1",), b)
                    sp.dma_start(x_in[k][:], x_d[b.value(1, 3)]).then_inc(x_loaded[k], 16)
                if store:
                    wait_read(sp, ("down2",), b)
                    sp.dma_start(out_d[b.value(1, -1)], y_out[:]).then_inc(stored, 16)

            load_and_store(Batch(-1), True, False)
            load_and_store(Batch(0), True, False)
            with sp.Fori(0, (B - 4) // 2) as turn:
                for b in (1, 2):
                    load_and_store(Batch(b, turn), True, True)
            for b in range(B - 3, B + 1):
                load_and_store(Batch(b), False, True)
            sp.wait_ge(stored, 16 * B)

        @block.gpsimd
        def _(pool):
            nc.gpsimd.memset(ident[:], 0.0).then_inc(ident_zero, 1)
            pool.wait_ge(ident_zero, 1)
            nc.gpsimd.affine_select(out=ident[:], in_=ident[:], compare_op=ALU.not_equal, fill=1.0, base=0,
                                    pattern=[[-1, P]], channel_multiplier=1).then_inc(ident_ready, 1)
            for k in range(2):
                nc.gpsimd.memset(q_parts[k][:, :, :, ROWS_MAX:STRIP], 0.0).then_inc(parts_set, 1)
                nc.gpsimd.memset(k_parts[k][:, :, :, ROWS_MAX:ROWS_EXP], 1.0).then_inc(parts_set, 1)
                nc.gpsimd.memset(k_parts[k][:, :, :, ROWS_EXP:STRIP], 0.0).then_inc(parts_set, 1)
                nc.gpsimd.memset(v_aug[k][:, :, :, D:D + 1], 1.0).then_inc(parts_set, 1)
                nc.gpsimd.memset(v_aug[k][:, :, :, D + 1:STRIP], 0.0).then_inc(parts_set, 1)
            nc.gpsimd.memset(minus_half[:], -0.5).then_inc(parts_set, 1)
            pool.wait_ge(parts_set, 11)
            pool.wait_ge(tables_in, 16 * 4)

            def rope_steps(b):
                k = (b.first + 1) % 2
                done = [0]

                def link(ins):
                    done[0] += 1
                    ins.then_inc(rope_part, 1)

                def linked(back=0):
                    pool.wait_ge(rope_part, b.value(9, 9 + done[0] - back))

                wait_read(pool, ("qkv_3",), b)
                src = qkv[k][:, :, 0:2 * C].rearrange("p t (h d) -> p t h d", d=D)
                ra = rot_a[:].rearrange("p t (h d) -> p t h d", d=D)
                rb = rot_b[:].rearrange("p t (h d) -> p t h d", d=D)
                link(nc.gpsimd.tensor_tensor(ra, src, cos_t[:].unsqueeze(2).broadcast_to([P, T, 2 * H, D]), ALU.mult))
                for e in range(2):
                    link(nc.gpsimd.tensor_tensor(
                        rb[:, :, :, e::2], src[:, :, :, 1 - e::2],
                        sin_t[:, :, e::2].unsqueeze(2).broadcast_to([P, T, 2 * H, D // 2]), ALU.mult))
                linked()
                link(nc.gpsimd.tensor_tensor(rot_a[:], rot_a[:], rot_b[:], ALU.add))
                linked()
                settle(pool)
                qr = rot_a[:, :, 0:C].rearrange("p t (h d) -> p t h d", d=D)
                kr = rot_a[:, :, C:2 * C].rearrange("p t (h d) -> p t h d", d=D)
                qp, kp = q_parts[k], k_parts[k]

                def part(tensor, n, dt=F32):
                    return tensor[:, :, :, n * D:(n + 1) * D].bitcast(dt)

                link(nc.gpsimd.tensor_copy(part(qp, 0, F32R), qr))
                link(nc.gpsimd.tensor_copy(part(kp, 0, F32R), kr))
                link(nc.gpsimd.tensor_copy(part(qp, 1, F32R), qr))
                link(nc.gpsimd.tensor_copy(part(kp, 2, F32R), kr))
                linked(back=2)
                link(nc.gpsimd.tensor_tensor(part(qp, 2, F32R), qr, part(qp, 0), ALU.subtract))
                nc.gpsimd.tensor_tensor(part(kp, 1, F32R), kr, part(kp, 0), ALU.subtract).then_inc(parts_ready, 1)

            def run(st, b):
                what = st[0]
                if what.startswith("stats"):
                    n = int(what[-1]) - 1
                    nb = b.value(1, 2) if n < 2 else b.value(1, 0)
                    pool.wait_ge(stats_ready[n], nb)
                    settle(pool)
                    nc.gpsimd.tensor_scalar(var_eps[n][:], mean_var[n][:, :, 1], EPS, None, ALU.add).then_inc(var_ready, 1)
                    pool.wait_ge(var_ready, b.counted(STAT, st, plus=1))
                    nc.gpsimd.tensor_tensor(rstd[n][:], var_eps[n][:], minus_half[:], ALU.pow).then_inc(rstd_ready[n], 1)
                elif what == "rope":
                    rope_steps(b)
                elif what == "vAug":
                    nb, ng = slot(b, st[1] + 1)
                    if ng == 0:
                        wait_read(pool, ("qkv_3",), b)
                    wait(pool, pv_done, nb.value(GROUPS, ng - 1))
                    settle(pool)
                    v = qkv[nb.first % 2][:, :, 2 * C + 4 * D * ng:2 * C + 4 * D * (ng + 1)]
                    nc.gpsimd.tensor_copy(v_aug[ng % 2][:, :, :, 0:D],
                                          v.rearrange("p t (h d) -> p t h d", d=D)).then_inc(v_ready, 1)

            program(run, pool)

        @block.scalar
        def _(act):
            act.wait_ge(setup_T, 4)
            nc.scalar.copy(w_gateT[:], max_ps[0][:, 0:HID]).then_inc(weights_ready, 1)
            nc.scalar.copy(w_upT[:], max_ps[1][:, 0:HID]).then_inc(weights_ready, 1)
            nc.scalar.mul(w_downT[:], exp_ps[0][:, 0:HID].rearrange("p (j c) -> p j c", j=J), 0.25).then_inc(weights_ready, 1)
            nc.scalar.mul(w_qkvT[:, 0:C], exp_ps[1][:, 0:C], Q_SCALE).then_inc(weights_ready, 1)
            nc.scalar.copy(w_qkvT[:, C:3 * C], exp_ps[1][:, C:3 * C]).then_inc(weights_ready, 1)
            nc.scalar.copy(w_projT[:], exp_ps[1][:, 3 * C:4 * C]).then_inc(weights_ready, 1)

            def take(dst, st, b):
                wait_dense(act, st, b)
                k = bank(st, b)
                nc.scalar.copy(dst, dense_ps[k][:]).then_inc(dense_read[k], 1)

            def run(st, b):
                what = st[0]
                if what == "exp":
                    g, i = st[1:]
                    if i == 0:
                        wait(act, pv_done, b.value(GROUPS, g - 1))
                    wait(act, expscore_ready, b.value(GROUPS * TILES, TILES * g + i + 1))
                    nc.scalar.activation(probs[g % 2][:, i // T, i % T, :], exp_ps[i % 2][:], ACT.Exp).then_inc(exp_done, 1)
                elif what == "kT":
                    take(kT[(st[1] + 1) % 2][:], st, b)
                elif what == "qT":
                    take(qT[:], st, b)
                elif what == "qmT":
                    take(qmT[(st[1] + 1) % 2][:], st, b)
                elif what in ("xT1", "xT2", "xT3"):
                    take(x_hatT[int(what[-1]) - 1][:], st, b)
                elif what == "attnT":
                    take(attnT[:], st, b)
                elif what == "oCopy":
                    pb, pg = slot(b, st[1] - 1)
                    wait(act, pv_done, pb.value(GROUPS, pg + 1))
                    if (("oT", pg), pb.first) in USE:
                        wait_dense(act, ("oT", pg), pb)
                    nc.scalar.copy(oT[:], pv_ps[:]).then_inc(o_copied, 1)
                elif what.startswith("gate"):
                    wait_dense(act, st, b)
                    n, j = int(what[4]) - 1, int(what[-1])
                    if b.turn is not None:
                        wait(act, max_done, b.value(GROUPS * TILES, TILES * ((0, 2)[n] + 1)))
                    elif (st, b.first - 1) in USE:
                        wait_read(act, st, Batch(b.first - 1))
                    nc.scalar.activation(tanh[n][:, j, :], dense_ps[bank(st, b)][:], ACT.Tanh, scale=0.5).then_inc(tanh_ready, 1)

            program(run, act)

        @block.vector
        def _(dve):
            dve.wait_ge(weights_in, 16 * 5)
            nc.vector.tensor_scalar(rows_ffn[:].rearrange("p j c -> p (j c)"), rows_int[:], W_SCALE, None,
                                    ALU.mult).then_inc(dequantized, 1)
            dve.wait_ge(tables_in, 16 * 4)
            nc.vector.tensor_scalar(b_qkv[:, 0:C], b_qkv[:, 0:C], Q_SCALE, None, ALU.mult).then_inc(dequantized, 1)
            dve.wait_ge(dequantized, 2)

            def layer_stats(n, src, b, nb):
                for t in range(T):
                    nc.vector.bn_stats(stats[n][:, t, :], src[:, t, :]).then_inc(stats_part, 1)
                dve.wait_ge(stats_part, b.counted(STAT, (f"stats{n + 1}",), plus=1) * T)
                settle(dve)
                for t in range(T):
                    ins = nc.vector.bn_aggr(mean_var[n][:, t, :], stats[n][:, t, :])
                ins.then_inc(stats_ready[n], 1)

            def run(st, b):
                what = st[0]
                ahead = (b.first + 1) % 2
                k = bank(st, b) if what in DENSE_USERS else None
                if what == "max":
                    nb, ng = slot(b, st[1] + 1)
                    wait(dve, maxscore_ready, nb.value(GROUPS * TILES, TILES * ng + st[2] + 1))
                    nc.vector.tensor_reduce(neg_max[ng % 2][:, st[2] // T, st[2] % T:st[2] % T + 1], max_ps[st[2] % 2][:],
                                            AX_X, ALU.max, negate=True).then_inc(max_done, 1)
                elif what == "negMax":
                    nb, ng = slot(b, st[1] + 1)
                    wait(dve, max_done, nb.value(GROUPS * TILES, TILES * (ng + 1)))
                    m = neg_max[ng % 2][:].rearrange("p h t -> p t h")
                    q = q_parts[nb.first % 2][:, :, 4 * ng:4 * ng + 4, :]
                    nc.vector.tensor_copy(q[:, :, :, ROWS_MAX].bitcast(F32R), m).then_inc(negmax_hi, 1)
                    wait(dve, negmax_hi, nb.value(GROUPS, ng + 1))
                    nc.vector.tensor_tensor(q[:, :, :, ROWS_MAX + 1].bitcast(F32R), m, q[:, :, :, ROWS_MAX],
                                            ALU.subtract).then_inc(negmax_ready, 1)
                elif what == "oT":
                    pb, pg = slot(b, st[1] - 1)
                    o = dense_ps[k][:].rearrange("p (t h r) -> p t h r", t=T, r=STRIP)
                    wait_dense(dve, st, b)
                    nc.vector.reciprocal(recip[pg % 2][:], o[:, :, :, D]).then_inc(recip_done, 1)
                    wait(dve, recip_done, pb.value(GROUPS, pg + 1))
                    a = attn[pb.first % 2][:, :, 4 * D * pg:4 * D * (pg + 1)].rearrange("p t (h d) -> p t h d", d=D)
                    nc.vector.tensor_tensor(a, o[:, :, :, 0:D], recip[pg % 2][:].unsqueeze(3).broadcast_to([P, T, 4, D]),
                                            ALU.mult).then_inc(dense_read[k], 1)
                elif what.startswith("gate"):
                    n = GATE[st, b.first]
                    wait(dve, tanh_ready, b.counted(GATE, st, plus=1))
                    nc.vector.scalar_tensor_tensor(silu[n % 2][:], tanh[int(what[4]) - 1][:, int(what[-1]), :], 1.0, dense_ps[k][:], ALU.add,
                                                   ALU.mult).then_inc(dense_read[k], 1)
                elif what.startswith("up"):
                    g_st = (what.replace("up", "gate"),)
                    n = GATE[g_st, b.first]
                    wait_dense(dve, st, b)
                    wait_read(dve, g_st, b)
                    nc.vector.tensor_tensor(hid[:, int(what[-1]), :], silu[n % 2][:], dense_ps[k][:],
                                            ALU.mult).then_inc(dense_read[k], 1)
                elif what == "stats1":
                    dve.wait_ge(x_loaded[ahead], b.value(8, 24 if ahead == 0 else 16))
                    layer_stats(0, x_in[ahead], b, 1)
                elif what == "stats2":
                    wait_read(dve, ("down1",), b)
                    layer_stats(1, x_ffn1[ahead], b, 1)
                elif what == "stats3":
                    wait_read(dve, ("proj",), b)
                    layer_stats(2, x_attn, b, -1)
                elif what.startswith("norm"):
                    n = int(what[-1]) - 1
                    src = (x_in[ahead], x_ffn1[ahead], x_attn)[n]
                    dve.wait_ge(rstd_ready[n], b.value(1, 2) if n < 2 else b.value(1, 0))
                    for t in range(T):
                        ins = nc.vector.tensor_scalar(x_hat[n][:, t, :], src[:, t, :], mean_var[n][:, t, 0:1],
                                                      rstd[n][:, t:t + 1], ALU.subtract, ALU.mult)
                    ins.then_inc(hat_ready[n], 1)
                elif what == "down1":
                    wait_dense(dve, st, b)
                    nc.vector.tensor_tensor(x_ffn1[ahead][:].rearrange("p t c -> p (t c)"), dense_ps[k][:],
                                            x_in[ahead][:].rearrange("p t c -> p (t c)"), ALU.add).then_inc(dense_read[k], 1)
                elif what.startswith("qkv"):
                    wait_dense(dve, st, b)
                    nc.vector.tensor_tensor(qkv[ahead][:, int(what[-1]), :], dense_ps[k][:, 0:3 * C], b_qkv[:],
                                            ALU.add).then_inc(dense_read[k], 1)
                elif what == "proj":
                    wait_dense(dve, st, b)
                    nc.vector.tensor_tensor(x_attn[:].rearrange("p t c -> p (t c)"), dense_ps[k][:],
                                            x_ffn1[ahead][:].rearrange("p t c -> p (t c)"), ALU.add).then_inc(proj_part, 1)
                    dve.wait_ge(proj_part, b.value(1, 0))
                    nc.vector.tensor_tensor(x_attn[:], x_attn[:], b_proj[:].unsqueeze(1).broadcast_to([P, T, C]),
                                            ALU.add).then_inc(dense_read[k], 1)
                elif what == "down2":
                    wait_dense(dve, st, b)
                    wait(dve, stored, b.value(16, -16))
                    nc.vector.tensor_tensor(y_out[:].rearrange("p t c -> p (t c)"), dense_ps[k][:],
                                            x_attn[:].rearrange("p t c -> p (t c)"), ALU.add).then_inc(dense_read[k], 1)

            program(run, dve)

        @block.tensor
        def _(pe):
            pe.wait_ge(ident_ready, 1)
            pe.wait_ge(dequantized, 2)
            pe.wait_ge(weights_in, 16 * 5)
            for n, dst, src in ((J, max_ps[0], [rows_ffn[:, j, :] for j in range(J)]),
                                (J, max_ps[1], [rows_ffn[:, J + j, :] for j in range(J)]),
                                (J, exp_ps[0], [rows_ffn[:, 2 * J + j, :] for j in range(J)]),
                                (4, exp_ps[1], [rows_qkv[:, j, :] for j in range(4)])):
                for j in range(n):
                    ins = nc.tensor.transpose(dst[:, tile(j)], src[j], ident[:])
                ins.then_inc(setup_T, 1)
            pe.wait_ge(weights_ready, 6)
            pe.wait_ge(parts_set, 11)

            def transposes(st, b, src):
                k = bank(st, b)
                for t in range(T):
                    ins = nc.tensor.transpose(dense_ps[k][:, tile(t)], src(t), ident[:])
                ins.then_inc(dense_ready, 1)

            def run(st, b):
                what = st[0]
                ahead = (b.first + 1) % 2
                if what in DENSE_USERS:
                    k = bank(st, b)
                    wait(pe, dense_read[k], b.counted(USE, st, per=N_DENSE))
                if what in ("kT", "qT"):
                    nb, ng = slot(b, st[1] + 1)
                    wait(pe, parts_ready, nb.value(1, 1))
                    src = (k_parts if what == "kT" else q_parts)[nb.first % 2]
                    transposes(st, b, lambda t: src[:, t, 4 * ng:4 * ng + 4, :].rearrange("p h r -> p (h r)"))
                elif what == "qmT":
                    nb, ng = slot(b, st[1] + 1)
                    wait(pe, negmax_ready, nb.value(GROUPS, ng + 1))
                    transposes(st, b, lambda t: q_parts[nb.first % 2][:, t, 4 * ng:4 * ng + 4, :].rearrange("p h r -> p (h r)"))
                elif what == "exp":
                    g, i = st[1:]
                    hs, t = divmod(i, T)
                    if i == 0:
                        pb, pg = slot(b, g - 1)
                        wait_read(pe, ("qmT", pg), pb)
                    wait(pe, exp_done, b.value(GROUPS * TILES, TILES * g + i - 1))
                    rows = head_strip(hs, ROWS_EXP)
                    nc.tensor.matmul(exp_ps[i % 2][:], kT[g % 2][rows, tile(t)], qmT[g % 2][rows, :],
                                     start=True, stop=True).then_inc(expscore_ready, 1)
                elif what == "max":
                    nb, ng = slot(b, st[1] + 1)
                    hs, t = divmod(st[2], T)
                    if st[2] == 0:
                        wait_read(pe, ("kT", st[1]), b)
                        wait_read(pe, ("qT", st[1]), b)
                    wait(pe, max_done, nb.value(GROUPS * TILES, TILES * ng + st[2] - 1))
                    rows = head_strip(hs, ROWS_MAX)
                    nc.tensor.matmul(max_ps[st[2] % 2][:], qT[rows, tile(t)], kT[ng % 2][rows, :],
                                     start=True, stop=True).then_inc(maxscore_ready, 1)
                elif what == "pv":
                    pb, pg = slot(b, st[1] - 1)
                    t = st[2]
                    if t == 0:
                        wait(pe, exp_done, pb.value(GROUPS * TILES, TILES * (pg + 1)))
                        wait(pe, v_ready, pb.value(GROUPS, pg + 1))
                        wait(pe, o_copied, pb.value(GROUPS, pg))
                    for hs in range(4):
                        ins = nc.tensor.matmul(pv_ps[head_strip(hs), :], v_aug[pg % 2][:, t, hs, :],
                                               probs[pg % 2][:, hs, t, :], start=(t == 0), stop=(t == T - 1))
                    if t == T - 1:
                        ins.then_inc(pv_done, 1)
                elif what == "oT":
                    pb, pg = slot(b, st[1] - 1)
                    wait(pe, o_copied, pb.value(GROUPS, pg + 1))
                    transposes(st, b, lambda t: oT[:, tile(t)])
                elif what in ("xT1", "xT2", "xT3"):
                    n = int(what[-1]) - 1
                    pe.wait_ge(hat_ready[n], b.value(1, 2) if n < 2 else b.value(1, 0))
                    transposes(st, b, lambda t: x_hat[n][:, t, :])
                elif what.startswith(("gate", "up")):
                    n, j = int(what[-3]) - 1, int(what[-1])
                    if j == 0 and what.startswith("gate"):
                        wait_read(pe, (("xT1",), ("xT3",))[n], b)
                    w = w_gateT if what.startswith("gate") else w_upT
                    nc.tensor.matmul(dense_ps[k][:], w[:, tile(j)], x_hatT[(0, 2)[n]][:],
                                     start=True, stop=True).then_inc(dense_ready, 1)
                elif what in ("down1", "down2"):
                    n = int(what[-1]) - 1
                    wait_read(pe, (f"up{n + 1}_{J - 1}",), b)
                    for t in range(T):
                        for j in range(J):
                            ins = nc.tensor.matmul(dense_ps[k][:, tile(t)], hid[:, j, tile(t)], w_downT[:, j, :],
                                                   start=(j == 0), stop=(j == J - 1))
                    ins.then_inc(dense_ready, 1)
                elif what.startswith("qkv"):
                    if what == "qkv_0":
                        wait_read(pe, ("xT2",), b)
                    nc.tensor.matmul(dense_ps[k][:, 0:3 * C], x_hatT[1][:, tile(int(what[-1]))], w_qkvT[:],
                                     start=True, stop=True).then_inc(dense_ready, 1)
                elif what == "attnT":
                    wait_read(pe, ("oT", 0), b)
                    transposes(st, b, lambda t: attn[ahead][:, t, :])
                elif what == "proj":
                    wait_read(pe, ("attnT",), b)
                    for t in range(T):
                        ins = nc.tensor.matmul(dense_ps[k][:, tile(t)], attnT[:, tile(t)], w_projT[:],
                                               start=True, stop=True)
                    ins.then_inc(dense_ready, 1)

            program(run, pe)


_INS = ["L0_attn_x", "L0_attn_qkv_w", "L0_attn_qkv_b", "L0_attn_proj_w", "L0_attn_proj_b",
        "L0_ffn_w_gate", "L0_ffn_w_up", "L0_ffn_w_down"]


def rope_tables():
    import numpy as np

    inv_freq = (np.float32(1.0) / np.float32(10000.0) ** (np.arange(0, D, 2, dtype=np.float32) / np.float32(D))).astype(np.float32)
    freqs = np.arange(L, dtype=np.float32)[:, None] * inv_freq[None, :]
    angle = np.concatenate([freqs, freqs], axis=-1).astype(np.float64)
    sign = np.where(np.arange(D) % 2 == 0, -1.0, 1.0)
    return np.cos(angle).astype(np.float32), (np.sin(angle) * sign).astype(np.float32)


def kernel(**inputs):
    import numpy as np
    import concourse.bacc as bacc
    from concourse.bass_utils import run_bass_kernel_spmd

    nc = bacc.Bacc("TRN2", target_bir_lowering=False, num_devices=1)
    arrays = {name: np.ascontiguousarray(inputs[name]) for name in _INS}
    arrays["rope_cos"], arrays["rope_sin"] = rope_tables()
    args = [nc.dram_tensor(name, a.shape, mybir.dt.from_np(a.dtype), kind="ExternalInput").ap()
            for name, a in arrays.items()]
    out = nc.dram_tensor("out", (B, L, C), F32, kind="ExternalOutput").ap()
    macaron_layer(nc, *args, out)
    result = run_bass_kernel_spmd(nc, [arrays], core_ids=[0])
    return result.results[0]["out"]
```

```python
from contextlib import ExitStack

import concourse.bass as bass
from concourse import mybir

F32 = mybir.dt.float32
F32R = mybir.dt.float32r
I32 = mybir.dt.int32
ALU = mybir.AluOpType
ACT = mybir.ActivationFunctionType
AX_X = mybir.AxisListType.X

P = 128
B, L, C = 16, 512, 128
H, D = 16, 8
T = L // P
HID = 384
J = HID // P
GROUPS = H // 4
STRIP = 32
PARTS = 4
MAX_ROW = PARTS - 1
TILES = 4 * T
LEAD = 9
SLOTS = B * GROUPS
EPS = 1e-5
W_SCALE = 1.0 / 127.0
Q_SCALE = float(D) ** -0.5
N_DENSE = 3

EVERY_SLOT = {1: ["pv_0"], 4: ["pv_1"], 7: ["pv_2", "negMax"], 9: ["maxT"], 10: ["pv_3", "maxRows"],
              11: ["oCopy"], 12: ["oT"], 13: ["vAug"], 14: ["oDiv"]}
BY_GROUP = [
    {0: ["load", "down1_0"], 1: ["down1_1"], 2: ["down1_2"], 3: ["down1_3"], 4: ["ffn1"], 5: ["stats2_0"],
     6: ["stats2_1"], 7: ["aggr2", "norm2"], 14: ["xT2"], 15: ["qkv_0"]},
    {1: ["qkv_1"], 2: ["qkv_2"], 3: ["qkv_3"], 4: ["rope"], 5: ["attnT"], 6: ["proj"], 8: ["attnAdd"],
     9: ["stats3_0"], 10: ["stats3_1"], 11: ["aggr3", "norm3", "res"]},
    {0: ["kT"], 1: ["kSplit"], 2: ["qT"], 3: ["qSplit", "place", "xT3"], 4: ["gate2_0"], 5: ["silu2_0", "stats1_0"], 6: ["up2_0"],
     7: ["hid2_0", "gate2_1", "stats1_1"], 8: ["silu2_1", "up2_1", "aggr1", "norm1"], 9: ["hid2_1"], 10: ["gate2_2"],
     11: ["silu2_2", "up2_2"], 12: ["hid2_2"], 13: ["down2_0"], 15: ["down2_1"]},
    {0: ["down2_2"], 2: ["down2_3"], 3: ["ffn2", "store"], 5: ["xT1"], 6: ["gate1_0"], 7: ["silu1_0"], 8: ["up1_0"],
     9: ["hid1_0", "gate1_1"], 10: ["silu1_1", "up1_1"], 11: ["hid1_1"], 12: ["gate1_2"], 13: ["silu1_2", "up1_2"],
     14: ["hid1_2"]},
]
TWO_AHEAD = ("load", "stats1", "aggr1", "norm1", "xT1", "gate1", "silu1", "up1", "hid1")
ONE_AHEAD = ("down1", "ffn1", "stats2", "aggr2", "norm2", "res", "xT2", "qkv", "rope",
             "kT", "kSplit", "qT", "qSplit", "place")


def steps(b):
    out = []

    def exists(slot):
        return 0 <= slot < SLOTS

    for g in range(GROUPS):
        s = GROUPS * b + g
        for i in range(TILES):
            if exists(s):
                out.append(("exp", g, i))
            for what in BY_GROUP[g].get(i, []):
                kind = what.split("_")[0]
                ahead = 2 if kind in TWO_AHEAD else 1 if kind in ONE_AHEAD else -1
                if 0 <= b + ahead < B:
                    out.append((what,))
            if exists(s + (i + LEAD) // TILES + 1):
                out.append(("max", g, i + LEAD))
            for what in EVERY_SLOT.get(i, []):
                if exists(s - 1 if what in ("pv_0", "pv_1", "pv_2", "pv_3", "oCopy", "oT", "oDiv") else s + 1):
                    out.append((what, g))
    return out


DENSE_USERS = ("maxT", "oT", "xT1", "xT2", "xT3", "kT", "qT", "attnT", "proj", "down1_0", "down2_0",
               "qkv_0", "qkv_1", "qkv_2", "qkv_3") + tuple(
                   f"{k}{f}_{j}" for k in ("gate", "up") for f in (1, 2) for j in range(J))
SPLITS = ("xT1", "xT3", "kT", "qT")
FIRST, LAST = 1, 12


def number_uses():
    use, gate, stat, split = {}, {}, {}, {}
    for b in range(-2, B + 1):
        for st in steps(b):
            for table, member in ((use, st[0] in DENSE_USERS), (gate, st[0].startswith("gate")),
                                  (stat, st[0].startswith("aggr")), (split, st[0] in SPLITS)):
                if member:
                    table[st, b] = len(table)
    return use, gate, stat, split


class Batch:

    def __init__(self, first, turn=None):
        self.first, self.turn = first, turn

    def value(self, per_batch, plus):
        v = per_batch * self.first + plus
        return v if self.turn is None else self.turn * (2 * per_batch) + v

    def counted(self, table, key, per=1, plus=0):
        v = table[key, self.first]
        if self.turn is None:
            return v // per + plus
        grow = table[key, self.first + 2] - v
        assert grow % per == 0 and grow == table[key, self.first + 4] - table[key, self.first + 2]
        return self.turn * (grow // per) + (v // per + plus)


def macaron_layer(nc, x, qkv_w, qkv_b, proj_w, proj_b, w_gate, w_up, w_down, rope_cos, rope_sin, out):
    USE, GATE, STAT, SPLIT = number_uses()
    with ExitStack() as ctx:
        def sb(name, shape, dt=F32):
            return ctx.enter_context(nc.sbuf_tensor(name, shape, dt))

        def ps(name):
            return ctx.enter_context(nc.psum_tensor(name, [P, L], F32))

        def sem(name):
            return ctx.enter_context(nc.semaphore(name))

        ident = sb("ident", [P, P])
        ones = sb("ones", [8, L], F32R)
        zeros = sb("zeros", [8, L], F32R)
        cos_t = sb("cos_t", [P, T, D])
        sin_t = sb("sin_t", [P, T, D])
        probs = [sb(f"probs{k}", [P, 4, T, L]) for k in range(2)]
        rows_int = probs[1][:, 0, :, :].rearrange("p t q -> p (t q)")[:, 0:3 * HID].bitcast(I32)
        rows_ffn = probs[1][:, 1, :, :].rearrange("p t q -> p (t q)")[:, 0:3 * HID]
        rows_qkv = probs[1][:, 2, 0, :]
        w_hi = {k: sb(f"w_{k}_hi", [P, HID], F32R) for k in ("gate", "up")}
        w_lo = {k: sb(f"w_{k}_lo", [P, HID], F32R) for k in ("gate", "up")}
        w_downT = sb("w_downT", [P, J, C])
        w_qkvT = sb("w_qkvT", [P, 3 * C])
        w_projT = sb("w_projT", [P, C])
        b_qkv = sb("b_qkv", [P, 3 * C])
        b_proj = sb("b_proj", [P, C])
        minus_half = sb("minus_half", [P, T])
        x_in = [sb(f"x_in{k}", [P, T, C]) for k in range(2)]
        x_ffn1 = sb("x_ffn1", [P, T, C])
        x_res = [sb(f"x_res{k}", [P, T, C]) for k in range(2)]
        x_attn = sb("x_attn", [P, T, C])
        y_out = sb("y_out", [P, T, C])
        stats = [sb(f"stats{k}", [P, T, 6]) for k in range(3)]
        mean_var = [sb(f"mean_var{k}", [P, T, 2]) for k in range(3)]
        var_eps = [sb(f"var_eps{k}", [P, T]) for k in range(3)]
        rstd = [sb(f"rstd{k}", [P, T]) for k in range(3)]
        x_hat = [sb(f"x_hat{k}", [P, T, C]) for k in range(3)]
        xT_hi = {n: sb(f"xT{n}_hi", [P, L], F32R) for n in (1, 3)}
        xT_lo = {n: sb(f"xT{n}_lo", [P, L], F32R) for n in (1, 3)}
        xT_2 = sb("xT_2", [P, L])
        tanh = sb("tanh", [P, J, L])
        silu = [sb(f"silu{k}", [P, L]) for k in range(2)]
        hid = sb("hid", [P, J, L])
        qkv = [sb(f"qkv{k}", [P, T, 3 * C]) for k in range(2)]
        rot_a = sb("rot_a", [P, T, 2 * C])
        rot_b = sb("rot_b", [P, T, 2 * C])
        hi = {k: sb(f"{k}_hi", [P, L], F32R) for k in "qk"}
        lo = {k: sb(f"{k}_lo", [P, L], F32R) for k in "qk"}
        operand = {k: [sb(f"{k}_op{n}", [P, GROUPS, L], F32R) for n in range(2)] for k in "qk"}
        v_aug = [sb(f"v_aug{k}", [P, T, 4, STRIP]) for k in range(2)]
        neg_max = [sb(f"neg_max{k}", [P, T, 4]) for k in range(2)]
        max_parts = [sb(f"max_parts{k}", [P, T, 8]) for k in range(2)]
        max_rows = [sb(f"max_rows{k}", [8, L], F32R) for k in range(2)]
        oT = sb("oT", [P, L])
        recip = [sb(f"recip{k}", [P, T, 4]) for k in range(2)]
        attn = [sb(f"attn{k}", [P, T, C]) for k in range(2)]
        attnT = sb("attnT", [P, L])
        max_ps = [ps(f"max_ps{k}") for k in range(2)]
        exp_ps = [ps(f"exp_ps{k}") for k in range(2)]
        pv_ps = ps("pv_ps")
        dense_ps = [ps(f"dense_ps{k}") for k in range(N_DENSE)]

        weights_in = sem("weights_in")
        tables_in = sem("tables_in")
        ident_zero = sem("ident_zero")
        ident_ready = sem("ident_ready")
        set_once = sem("set_once")
        ones_placed = sem("ones_placed")
        dequantized = sem("dequantized")
        setup_T = sem("setup_T")
        weights_ready = sem("weights_ready")
        weights_lo = sem("weights_lo")
        x_loaded = [sem(f"x_loaded{k}") for k in range(2)]
        stored = sem("stored")
        dense_ready = sem("dense_ready")
        dense_read = [sem(f"dense_read{k}") for k in range(N_DENSE)]
        tanh_ready = sem("tanh_ready")
        hi_ready = sem("hi_ready")
        stats_part = sem("stats_part")
        stats_ready = [sem(f"stats_ready{k}") for k in range(3)]
        var_ready = sem("var_ready")
        rstd_ready = [sem(f"rstd_ready{k}") for k in range(3)]
        hat_ready = [sem(f"hat_ready{k}") for k in range(3)]
        res_ready = sem("res_ready")
        rope_part = sem("rope_part")
        rot_ready = sem("rot_ready")
        bias_v = sem("bias_v")
        placed = [sem(f"placed{g}") for g in range(GROUPS)]
        v_ready = sem("v_ready")
        maxscore_ready = sem("maxscore_ready")
        max_done = sem("max_done")
        negmax_hi = sem("negmax_hi")
        negmax_ready = sem("negmax_ready")
        maxrows_placed = [sem(f"maxrows_placed{k}") for k in range(2)]
        expscore_ready = sem("expscore_ready")
        exp_done = sem("exp_done")
        pv_done = sem("pv_done")
        o_copied = sem("o_copied")
        recip_done = sem("recip_done")
        passed = sem("passed")

        SET_ONCE = 11
        PLACE_DMAS = 7

        def wait(eng, s, value):
            if not (isinstance(value, int) and value <= 0):
                eng.wait_ge(s, value)

        def settle(eng):
            eng.sem_inc(passed, 1)

        def wait_dense(eng, st, b):
            wait(eng, dense_ready, b.counted(USE, st, plus=1))

        def bank(st, b):
            return USE[st, b.first] % N_DENSE

        def wait_read(eng, st, b):
            wait(eng, dense_read[bank(st, b)], b.counted(USE, st, per=N_DENSE, plus=1))

        def slot(b, g):
            return Batch(b.first + g // GROUPS, b.turn), g % GROUPS

        def max_tile(b, st):
            return *slot(b, st[1] + 1 + st[2] // TILES), st[2] % TILES

        def head_strip(hs):
            return slice(STRIP * hs, STRIP * (hs + 1))

        def tile(t):
            return slice(t * P, (t + 1) * P)

        def flat(t):
            return t[:].rearrange("p t c -> p (t c)")

        def program(run, eng):
            for b in range(-2, FIRST):
                for st in steps(b):
                    run(st, Batch(b))
            with eng.Fori(0, (LAST - FIRST + 1) // 2) as turn:
                for b in (FIRST, FIRST + 1):
                    for st in steps(b):
                        run(st, Batch(b, turn))
            for b in range(LAST + 1, B + 1):
                for st in steps(b):
                    run(st, Batch(b))

        x_d = x.rearrange("b (p t) c -> b p t c", t=T)
        out_d = out.rearrange("b (p t) c -> b p t c", t=T)
        block = ctx.enter_context(nc.Block())

        @block.sync
        def _(sp):
            def move(dst, src):
                return sp.dma_start(dst.bitcast(F32), src.bitcast(F32))

            for b in range(2):
                sp.dma_start(x_in[b][:], x_d[b]).then_inc(x_loaded[b], 16)
            for dst, src in (
                (rows_int[:, 0:HID].rearrange("p (j c) -> p j c", j=J), w_gate.rearrange("(j p) c -> p j c", p=P)),
                (rows_int[:, HID:2 * HID].rearrange("p (j c) -> p j c", j=J), w_up.rearrange("(j p) c -> p j c", p=P)),
                (rows_int[:, 2 * HID:3 * HID], w_down),
                (rows_qkv[:, 0:3 * C].rearrange("p (j c) -> p j c", j=J), qkv_w.rearrange("(j p) c -> p j c", p=P)),
                (rows_qkv[:, 3 * C:4 * C], proj_w),
            ):
                sp.dma_start(dst, src).then_inc(weights_in, 16)
            sp.dma_start(b_qkv[:], qkv_b.unsqueeze(0).broadcast_to([P, 3 * C])).then_inc(tables_in, 16)
            sp.dma_start(b_proj[:], proj_b.unsqueeze(0).broadcast_to([P, C])).then_inc(tables_in, 16)
            sp.dma_start(cos_t[:], rope_cos.rearrange("(p t) d -> p t d", t=T)).then_inc(tables_in, 16)
            sp.dma_start(sin_t[:], rope_sin.rearrange("(p t) d -> p t d", t=T)).then_inc(tables_in, 16)
            sp.wait_ge(set_once, SET_ONCE)
            for n in range(2):
                move(operand["k"][n][MAX_ROW:P:16, :, :], ones[:].unsqueeze(1).broadcast_to([8, GROUPS, L])).then_inc(ones_placed, 16)

            def run(st, b):
                what = st[0]
                if what == "load":
                    if b.turn is None and b.first < 0:
                        return
                    wait(sp, hat_ready[1], b.value(1, 1))
                    n = b.first % 2
                    sp.dma_start(x_in[n][:], x_d[b.value(1, 2)]).then_inc(x_loaded[n], 16)
                elif what == "store":
                    wait_read(sp, ("down2_0",), b)
                    sp.dma_start(out_d[b.value(1, -1)], y_out[:]).then_inc(stored, 16)
                elif what == "place":
                    n = (b.first + 1) % 2
                    wait_read(sp, ("qT",), b)
                    for g in range(GROUPS):
                        for k, parts in (("q", (hi, hi, lo)), ("k", (hi, lo, hi))):
                            for part, src in enumerate(parts):
                                move(operand[k][n][part:P:PARTS, g, :], src[k][head_strip(g), :]).then_inc(placed[g], 16)
                        move(operand["q"][n][MAX_ROW:P:16, g, :], zeros[:]).then_inc(placed[g], 16)

            program(run, sp)
            sp.wait_ge(stored, 16 * B)

        @block.gpsimd
        def _(pool):
            nc.gpsimd.memset(ident[:], 0.0).then_inc(ident_zero, 1)
            pool.wait_ge(ident_zero, 1)
            nc.gpsimd.affine_select(out=ident[:], in_=ident[:], compare_op=ALU.not_equal, fill=1.0, base=0,
                                    pattern=[[-1, P]], channel_multiplier=1).then_inc(ident_ready, 1)
            nc.gpsimd.memset(minus_half[:], -0.5).then_inc(set_once, 1)
            nc.gpsimd.memset(ones[:].bitcast(F32), 1.0).then_inc(set_once, 1)
            nc.gpsimd.memset(zeros[:].bitcast(F32), 0.0).then_inc(set_once, 1)
            for n in range(2):
                nc.gpsimd.memset(operand["k"][n][:].bitcast(F32), 0.0).then_inc(set_once, 1)
                nc.gpsimd.memset(operand["q"][n][:].bitcast(F32), 0.0).then_inc(set_once, 1)
                nc.gpsimd.memset(v_aug[n][:, :, :, D:D + 1], 1.0).then_inc(set_once, 1)
                nc.gpsimd.memset(v_aug[n][:, :, :, D + 1:STRIP], 0.0).then_inc(set_once, 1)
            pool.wait_ge(set_once, SET_ONCE)
            pool.wait_ge(tables_in, 16 * 4)
            pool.wait_ge(dequantized, 2)

            def rope_steps(b):
                done = [0]

                def link(ins):
                    done[0] += 1
                    ins.then_inc(rope_part, 1)

                def linked():
                    pool.wait_ge(rope_part, b.value(4, 4 + done[0]))

                wait_read(pool, ("qkv_3",), b)
                buf = qkv[(b.first + 1) % 2]
                qk = buf[:, :, 0:2 * C]
                link(nc.gpsimd.tensor_tensor(qk, qk, b_qkv[:, 0:2 * C].unsqueeze(1).broadcast_to([P, T, 2 * C]), ALU.add))
                linked()
                src = qk.rearrange("p t (h d) -> p t h d", d=D)
                ra = rot_a[:].rearrange("p t (h d) -> p t h d", d=D)
                rb = rot_b[:].rearrange("p t (h d) -> p t h d", d=D)
                link(nc.gpsimd.tensor_tensor(ra, src, cos_t[:].unsqueeze(2).broadcast_to([P, T, 2 * H, D]), ALU.mult))
                for e in range(2):
                    link(nc.gpsimd.tensor_tensor(
                        rb[:, :, :, e::2], src[:, :, :, 1 - e::2],
                        sin_t[:, :, e::2].unsqueeze(2).broadcast_to([P, T, 2 * H, D // 2]), ALU.mult))
                linked()
                nc.gpsimd.tensor_tensor(rot_a[:], rot_a[:], rot_b[:], ALU.add).then_inc(rot_ready, 1)
                v = buf[:, :, 2 * C:3 * C]
                nc.gpsimd.tensor_tensor(v, v, b_qkv[:, 2 * C:3 * C].unsqueeze(1).broadcast_to([P, T, C]),
                                        ALU.add).then_inc(bias_v, 1)

            def run(st, b):
                what = st[0]
                if what.startswith("aggr"):
                    n = int(what[-1]) - 1
                    pool.wait_ge(stats_ready[n], b.value(1, (3, 2, 0)[n]))
                    settle(pool)
                    nc.gpsimd.tensor_scalar(var_eps[n][:], mean_var[n][:, :, 1], EPS, None, ALU.add).then_inc(var_ready, 1)
                    pool.wait_ge(var_ready, b.counted(STAT, st, plus=1))
                    nc.gpsimd.tensor_tensor(rstd[n][:], var_eps[n][:], minus_half[:], ALU.pow).then_inc(rstd_ready[n], 1)
                elif what.startswith("norm"):
                    n = int(what[-1]) - 1
                    src = (x_in[b.first % 2], x_ffn1, x_attn)[n]
                    pool.wait_ge(rstd_ready[n], b.value(1, (3, 2, 0)[n]))
                    settle(pool)
                    for t in range(T):
                        ins = nc.gpsimd.tensor_scalar(x_hat[n][:, t, :], src[:, t, :], mean_var[n][:, t, 0:1],
                                                      rstd[n][:, t:t + 1], ALU.subtract, ALU.mult)
                    ins.then_inc(hat_ready[n], 1)
                elif what == "res":
                    if b.first > 0:
                        wait_read(pool, ("proj",), b)
                    nc.gpsimd.tensor_tensor(x_res[(b.first + 1) % 2][:], x_ffn1[:],
                                            b_proj[:].unsqueeze(1).broadcast_to([P, T, C]),
                                            ALU.add).then_inc(res_ready, 1)
                elif what == "rope":
                    rope_steps(b)
                elif what == "vAug":
                    nb, ng = slot(b, st[1] + 1)
                    pool.wait_ge(bias_v, nb.value(1, 1))
                    wait(pool, pv_done, nb.value(GROUPS, ng - 1))
                    settle(pool)
                    v = qkv[nb.first % 2][:, :, 2 * C + 4 * D * ng:2 * C + 4 * D * (ng + 1)]
                    nc.gpsimd.tensor_copy(v_aug[ng % 2][:, :, :, 0:D],
                                          v.rearrange("p t (h d) -> p t h d", d=D)).then_inc(v_ready, 1)

            program(run, pool)

        @block.scalar
        def _(act):
            act.wait_ge(setup_T, 4)
            nc.scalar.copy(w_hi["gate"][:], max_ps[0][:, 0:HID]).then_inc(weights_ready, 1)
            nc.scalar.copy(w_hi["up"][:], max_ps[1][:, 0:HID]).then_inc(weights_ready, 1)
            nc.scalar.mul(w_downT[:], exp_ps[0][:, 0:HID].rearrange("p (j c) -> p j c", j=J), 0.25).then_inc(weights_ready, 1)
            nc.scalar.mul(w_qkvT[:, 0:C], exp_ps[1][:, 0:C], Q_SCALE).then_inc(weights_ready, 1)
            nc.scalar.copy(w_qkvT[:, C:3 * C], exp_ps[1][:, C:3 * C]).then_inc(weights_ready, 1)
            nc.scalar.copy(w_projT[:], exp_ps[1][:, 3 * C:4 * C]).then_inc(weights_ready, 1)

            def take(dst, st, b):
                wait_dense(act, st, b)
                k = bank(st, b)
                nc.scalar.copy(dst, dense_ps[k][:]).then_inc(dense_read[k], 1)

            def run(st, b):
                what = st[0]
                if what == "exp":
                    g, i = st[1:]
                    if i == 0:
                        wait(act, pv_done, b.value(GROUPS, g - 1))
                    wait(act, expscore_ready, b.value(GROUPS * TILES, TILES * g + i + 1))
                    nc.scalar.activation(probs[g % 2][:, i // T, i % T, :], exp_ps[i % 2][:], ACT.Exp).then_inc(exp_done, 1)
                elif what in SPLITS:
                    wait_dense(act, st, b)
                    if what in ("kT", "qT"):
                        wait(act, placed[GROUPS - 1], b.value(16 * PLACE_DMAS, 16 * PLACE_DMAS))
                    dst = xT_hi[int(what[-1])] if what[0] == "x" else hi[what[0]]
                    nc.scalar.copy(dst[:], dense_ps[bank(st, b)][:]).then_inc(hi_ready, 1)
                elif what == "xT2":
                    take(xT_2[:], st, b)
                elif what == "attnT":
                    take(attnT[:], st, b)
                elif what.startswith("qkv"):
                    wait_dense(act, st, b)
                    k = bank(st, b)
                    nc.scalar.copy(qkv[(b.first + 1) % 2][:, int(what[-1]), :], dense_ps[k][:, 0:3 * C]).then_inc(dense_read[k], 1)
                elif what == "maxT":
                    nb, ng = slot(b, st[1] + 1)
                    wait_dense(act, st, b)
                    wait(act, maxrows_placed[ng % 2], nb.value(32, 16 * (ng // 2)))
                    k = bank(st, b)
                    nc.scalar.copy(max_rows[ng % 2][:], dense_ps[k][0:8, :]).then_inc(dense_read[k], 1)
                elif what == "maxRows":
                    nb, ng = slot(b, st[1] + 1)
                    wait_read(act, ("maxT", st[1]), b)
                    act.dma_start(operand["q"][nb.first % 2][MAX_ROW:P:16, ng, :].bitcast(F32),
                                  max_rows[ng % 2][:].bitcast(F32)).then_inc(maxrows_placed[ng % 2], 16)
                elif what == "oCopy":
                    pb, pg = slot(b, st[1] - 1)
                    wait(act, pv_done, pb.value(GROUPS, pg + 1))
                    if (("oT", pg), pb.first) in USE:
                        wait_dense(act, ("oT", pg), pb)
                    nc.scalar.copy(oT[:], pv_ps[:]).then_inc(o_copied, 1)
                elif what.startswith("gate"):
                    wait_dense(act, st, b)
                    n, j = int(what[4]) - 1, int(what[-1])
                    if b.turn is not None:
                        wait_read(act, (f"gate{2 - n}_{j}",), Batch(b.first - n, b.turn))
                    elif GATE[st, b.first] >= J:
                        (last, lb), = [key for key, at in GATE.items() if at == GATE[st, b.first] - J]
                        wait_read(act, last, Batch(lb))
                    nc.scalar.activation(tanh[:, j, :], dense_ps[bank(st, b)][:], ACT.Tanh, scale=0.5).then_inc(tanh_ready, 1)

            program(run, act)

        @block.vector
        def _(dve):
            dve.wait_ge(weights_in, 16 * 5)
            nc.vector.tensor_scalar(rows_ffn, rows_int, W_SCALE, None,
                                    ALU.mult).then_inc(dequantized, 1)
            dve.wait_ge(tables_in, 16 * 4)
            nc.vector.tensor_scalar(b_qkv[:, 0:C], b_qkv[:, 0:C], Q_SCALE, None, ALU.mult).then_inc(dequantized, 1)
            dve.wait_ge(weights_ready, 2)
            for k, bank_of in (("gate", max_ps[0]), ("up", max_ps[1])):
                nc.vector.tensor_tensor(w_lo[k][:], bank_of[:, 0:HID], w_hi[k][:].bitcast(F32),
                                        ALU.subtract).then_inc(weights_lo, 1)

            def split_lo(dst, high, st, b):
                wait(dve, hi_ready, b.counted(SPLIT, st, plus=1))
                k = bank(st, b)
                nc.vector.tensor_tensor(dst[:], dense_ps[k][:], high[:].bitcast(F32), ALU.subtract).then_inc(dense_read[k], 1)

            def run(st, b):
                what = st[0]
                ahead = (b.first + 1) % 2
                k = bank(st, b) if what in DENSE_USERS else None
                if what == "max":
                    nb, ng, v = max_tile(b, st)
                    wait(dve, maxscore_ready, nb.value(GROUPS * TILES, TILES * ng + v + 1))
                    nc.vector.tensor_reduce(neg_max[ng % 2][:, v % T, v // T:v // T + 1], max_ps[v % 2][:],
                                            AX_X, ALU.max, negate=True).then_inc(max_done, 1)
                elif what == "negMax":
                    nb, ng = slot(b, st[1] + 1)
                    wait(dve, max_done, nb.value(GROUPS * TILES, TILES * (ng + 1)))
                    m = neg_max[ng % 2][:]
                    parts = max_parts[ng % 2][:].rearrange("p t (h x) -> p t h x", x=2)
                    nc.vector.tensor_copy(parts[:, :, :, 0].bitcast(F32R), m).then_inc(negmax_hi, 1)
                    wait(dve, negmax_hi, nb.value(GROUPS, ng + 1))
                    nc.vector.tensor_tensor(parts[:, :, :, 1].bitcast(F32R), m, parts[:, :, :, 0],
                                            ALU.subtract).then_inc(negmax_ready, 1)
                elif what == "oDiv":
                    pb, pg = slot(b, st[1] - 1)
                    st = ("oT", st[1])
                    k = bank(st, b)
                    o = dense_ps[k][:].rearrange("p (t h r) -> p t h r", t=T, r=STRIP)
                    wait_dense(dve, st, b)
                    nc.vector.reciprocal(recip[pg % 2][:], o[:, :, :, D]).then_inc(recip_done, 1)
                    wait(dve, recip_done, pb.value(GROUPS, pg + 1))
                    a = attn[pb.first % 2][:, :, 4 * D * pg:4 * D * (pg + 1)].rearrange("p t (h d) -> p t h d", d=D)
                    nc.vector.tensor_tensor(a, o[:, :, :, 0:D], recip[pg % 2][:].unsqueeze(3).broadcast_to([P, T, 4, D]),
                                            ALU.mult).then_inc(dense_read[k], 1)
                elif what in ("xT1", "xT3"):
                    split_lo(xT_lo[int(what[-1])], xT_hi[int(what[-1])], st, b)
                elif what in ("kSplit", "qSplit"):
                    split_lo(lo[what[0]], hi[what[0]], (f"{what[0]}T",), b)
                elif what.startswith("silu"):
                    g_st = (what.replace("silu", "gate"),)
                    n, k = GATE[g_st, b.first], bank(g_st, b)
                    wait(dve, tanh_ready, b.counted(GATE, g_st, plus=1))
                    nc.vector.scalar_tensor_tensor(silu[n % 2][:], tanh[:, int(what[-1]), :], 1.0,
                                                   dense_ps[k][:], ALU.add, ALU.mult).then_inc(dense_read[k], 1)
                elif what.startswith("hid"):
                    g_st, u_st = (what.replace("hid", "gate"),), (what.replace("hid", "up"),)
                    n, k = GATE[g_st, b.first], bank(u_st, b)
                    wait_dense(dve, u_st, b)
                    wait_read(dve, g_st, b)
                    nc.vector.tensor_tensor(hid[:, int(what[-1]), :], silu[n % 2][:], dense_ps[k][:],
                                            ALU.mult).then_inc(dense_read[k], 1)
                elif what.startswith("stats"):
                    n, half = int(what[5]) - 1, int(what[-1])
                    src = (x_in[b.first % 2], x_ffn1, x_attn)[n]
                    if half:
                        pass
                    elif n == 0:
                        wait(dve, x_loaded[b.first % 2], b.value(8, 32 if b.first % 2 == 0 else 24))
                    else:
                        wait_read(dve, (("down1_0",), ("proj",))[n - 1], b)
                    for t in (2 * half, 2 * half + 1):
                        nc.vector.bn_stats(stats[n][:, t, :], src[:, t, :]).then_inc(stats_part, 1)
                elif what.startswith("aggr"):
                    n = int(what[-1]) - 1
                    dve.wait_ge(stats_part, b.counted(STAT, st, plus=1) * T)
                    settle(dve)
                    for t in range(T):
                        ins = nc.vector.bn_aggr(mean_var[n][:, t, :], stats[n][:, t, :])
                    ins.then_inc(stats_ready[n], 1)
                elif what == "ffn1":
                    st = ("down1_0",)
                    k = bank(st, b)
                    wait_dense(dve, st, b)
                    wait(dve, res_ready, b.value(1, 1))
                    nc.vector.tensor_tensor(flat(x_ffn1), dense_ps[k][:], flat(x_in[ahead]), ALU.add).then_inc(dense_read[k], 1)
                elif what == "attnAdd":
                    st = ("proj",)
                    k = bank(st, b)
                    wait_dense(dve, st, b)
                    wait(dve, res_ready, b.value(1, 0))
                    nc.vector.tensor_tensor(flat(x_attn), dense_ps[k][:], flat(x_res[ahead]), ALU.add).then_inc(dense_read[k], 1)
                elif what == "ffn2":
                    st = ("down2_0",)
                    k = bank(st, b)
                    wait_dense(dve, st, b)
                    wait(dve, stored, b.value(16, -16))
                    nc.vector.tensor_tensor(flat(y_out), dense_ps[k][:], flat(x_attn), ALU.add).then_inc(dense_read[k], 1)

            program(run, dve)

        @block.tensor
        def _(pe):
            pe.wait_ge(ident_ready, 1)
            pe.wait_ge(dequantized, 2)
            pe.wait_ge(weights_in, 16 * 5)
            for n, dst, src in ((J, max_ps[0], rows_ffn[:, 0:HID]), (J, max_ps[1], rows_ffn[:, HID:2 * HID]),
                                (J, exp_ps[0], rows_ffn[:, 2 * HID:3 * HID]), (4, exp_ps[1], rows_qkv)):
                for j in range(n):
                    ins = nc.tensor.transpose(dst[:, tile(j)], src[:, tile(j)], ident[:])
                ins.then_inc(setup_T, 1)
            pe.wait_ge(weights_ready, 6)
            pe.wait_ge(weights_lo, 2)
            pe.wait_ge(set_once, SET_ONCE)
            pe.wait_ge(ones_placed, 16 * 2)

            def transposes(st, b, src):
                k = bank(st, b)
                for t in range(T):
                    ins = nc.tensor.transpose(dense_ps[k][:, tile(t)], src(t), ident[:])
                ins.then_inc(dense_ready, 1)

            def run(st, b):
                what = st[0]
                ahead = (b.first + 1) % 2
                if what in DENSE_USERS:
                    k = bank(st, b)
                    wait(pe, dense_read[k], b.counted(USE, st, per=N_DENSE))
                if what == "exp":
                    g, i = st[1:]
                    hs, t = divmod(i, T)
                    if i == 0:
                        pe.wait_ge(maxrows_placed[g % 2], b.value(32, 16 * (g // 2) + 16))
                    wait(pe, exp_done, b.value(GROUPS * TILES, TILES * g + i - 1))
                    n = b.first % 2
                    nc.tensor.matmul(exp_ps[i % 2][:], operand["k"][n][head_strip(hs), g, tile(t)],
                                     operand["q"][n][head_strip(hs), g, :],
                                     start=True, stop=True).then_inc(expscore_ready, 1)
                elif what == "max":
                    nb, ng, v = max_tile(b, st)
                    hs, t = divmod(v, T)
                    if v == 0:
                        pe.wait_ge(placed[ng], nb.value(16 * PLACE_DMAS, 16 * PLACE_DMAS))
                    wait(pe, max_done, nb.value(GROUPS * TILES, TILES * ng + v - 1))
                    n = nb.first % 2
                    nc.tensor.matmul(max_ps[v % 2][:], operand["q"][n][head_strip(hs), ng, tile(t)],
                                     operand["k"][n][head_strip(hs), ng, :],
                                     start=True, stop=True).then_inc(maxscore_ready, 1)
                elif what == "maxT":
                    nb, ng = slot(b, st[1] + 1)
                    wait(pe, negmax_ready, nb.value(GROUPS, ng + 1))
                    for t in range(T):
                        ins = nc.tensor.transpose(dense_ps[k][0:8, tile(t)], max_parts[ng % 2][:, t, :], ident[:])
                    ins.then_inc(dense_ready, 1)
                elif what.startswith("pv"):
                    pb, pg = slot(b, st[1] - 1)
                    t = int(what[-1])
                    if t == 0:
                        wait(pe, exp_done, pb.value(GROUPS * TILES, TILES * (pg + 1)))
                        wait(pe, v_ready, pb.value(GROUPS, pg + 1))
                        wait(pe, o_copied, pb.value(GROUPS, pg))
                    for hs in range(4):
                        ins = nc.tensor.matmul(pv_ps[head_strip(hs), :], v_aug[pg % 2][:, t, hs, :],
                                               probs[pg % 2][:, hs, t, :], start=(t == 0), stop=(t == T - 1))
                    if t == T - 1:
                        ins.then_inc(pv_done, 1)
                elif what == "oT":
                    pb, pg = slot(b, st[1] - 1)
                    wait(pe, o_copied, pb.value(GROUPS, pg + 1))
                    transposes(st, b, lambda t: oT[:, tile(t)])
                elif what in ("kT", "qT"):
                    pe.wait_ge(rot_ready, b.value(1, 2))
                    at = 0 if what == "qT" else C
                    transposes(st, b, lambda t: rot_a[:, t, at:at + C])
                elif what in ("xT1", "xT2", "xT3"):
                    n = int(what[-1]) - 1
                    pe.wait_ge(hat_ready[n], b.value(1, (3, 2, 0)[n]))
                    transposes(st, b, lambda t: x_hat[n][:, t, :])
                elif what.startswith(("gate", "up")):
                    n, j = {"1": 1, "2": 3}[what[-3]], int(what[-1])
                    w = what[:-3]
                    if j == 0 and w == "gate":
                        wait_read(pe, (f"xT{n}",), b)
                    for m, (a, c) in enumerate(((w_hi, xT_hi), (w_hi, xT_lo), (w_lo, xT_hi))):
                        ins = nc.tensor.matmul(dense_ps[k][:], a[w][:, tile(j)], c[n][:], start=(m == 0), stop=(m == 2))
                    ins.then_inc(dense_ready, 1)
                elif what.startswith("down"):
                    t = int(what[-1])
                    first = (what[:-1] + "0",)
                    k = bank(first, b)
                    if t == 0:
                        wait_read(pe, (f"up{what[4]}_{J - 1}",), Batch(b.first - 1, b.turn) if what[4] == "1" else b)
                    for j in range(J):
                        ins = nc.tensor.matmul(dense_ps[k][:, tile(t)], hid[:, j, tile(t)], w_downT[:, j, :],
                                               start=(j == 0), stop=(j == J - 1))
                    if t == T - 1:
                        ins.then_inc(dense_ready, 1)
                elif what.startswith("qkv"):
                    if what == "qkv_0":
                        wait_read(pe, ("xT2",), b)
                    nc.tensor.matmul(dense_ps[k][:, 0:3 * C], xT_2[:, tile(int(what[-1]))], w_qkvT[:],
                                     start=True, stop=True).then_inc(dense_ready, 1)
                elif what == "attnT":
                    wait_read(pe, ("oT", 0), b)
                    transposes(st, b, lambda t: attn[ahead][:, t, :])
                elif what == "proj":
                    wait_read(pe, ("attnT",), b)
                    for t in range(T):
                        ins = nc.tensor.matmul(dense_ps[k][:, tile(t)], attnT[:, tile(t)], w_projT[:],
                                               start=True, stop=True)
                    ins.then_inc(dense_ready, 1)

            program(run, pe)


_INS = ["L0_attn_x", "L0_attn_qkv_w", "L0_attn_qkv_b", "L0_attn_proj_w", "L0_attn_proj_b",
        "L0_ffn_w_gate", "L0_ffn_w_up", "L0_ffn_w_down"]


def rope_tables():
    import numpy as np

    inv_freq = (np.float32(1.0) / np.float32(10000.0) ** (np.arange(0, D, 2, dtype=np.float32) / np.float32(D))).astype(np.float32)
    freqs = np.arange(L, dtype=np.float32)[:, None] * inv_freq[None, :]
    angle = np.concatenate([freqs, freqs], axis=-1).astype(np.float64)
    sign = np.where(np.arange(D) % 2 == 0, -1.0, 1.0)
    return np.cos(angle).astype(np.float32), (np.sin(angle) * sign).astype(np.float32)


def kernel(**inputs):
    import numpy as np
    import concourse.bacc as bacc
    from concourse.bass_utils import run_bass_kernel_spmd

    nc = bacc.Bacc("TRN2", target_bir_lowering=False, num_devices=1)
    arrays = {name: np.ascontiguousarray(inputs[name]) for name in _INS}
    arrays["rope_cos"], arrays["rope_sin"] = rope_tables()
    args = [nc.dram_tensor(name, a.shape, mybir.dt.from_np(a.dtype), kind="ExternalInput").ap()
            for name, a in arrays.items()]
    out = nc.dram_tensor("out", (B, L, C), F32, kind="ExternalOutput").ap()
    macaron_layer(nc, *args, out)
    result = run_bass_kernel_spmd(nc, [arrays], core_ids=[0])
    return result.results[0]["out"]
```

```python
from contextlib import ExitStack

import concourse.bass as bass
from concourse import mybir

F32 = mybir.dt.float32
F32R = mybir.dt.float32r
I32 = mybir.dt.int32
ALU = mybir.AluOpType
ACT = mybir.ActivationFunctionType
AX_X = mybir.AxisListType.X

P = 128
B, L, C = 16, 512, 128
H, D = 16, 8
T = L // P
HID = 384
J = HID // P
GROUPS = H // 4
STRIP = 32
PARTS = 4
MAX_ROW = PARTS - 1
TILES = 4 * T
LEAD = 9
SLOTS = B * GROUPS
EPS = 1e-5
W_SCALE = 1.0 / 127.0
Q_SCALE = float(D) ** -0.5
N_DENSE = 3

EVERY_SLOT = {0: ["pv_0"], 1: ["oT"], 3: ["oDiv"], 4: ["pv_1"], 6: ["negHi"], 7: ["negLo"], 9: ["maxT"],
              10: ["pv_2", "maxRows"], 14: ["pv_3", "oCopy"], 15: ["vAug"]}
BY_GROUP = [
    {0: ["load", "gate2_0", "stats2_1"], 1: ["aggr2", "norm2"], 2: ["silu2_0"], 3: ["up2_0"],
     6: ["gate2_1", "hid2_0"], 7: ["silu2_1", "up2_1"], 8: ["hid2_1"], 9: ["gate2_2"], 10: ["silu2_2", "xT2"],
     12: ["up2_2", "qkv_0"], 13: ["qkv_1"], 14: ["hid2_2"], 15: ["qkv_2"]},
    {0: ["qkv_3"], 3: ["down2_0", "rope"], 4: ["down2_1"], 6: ["stats1_0"], 7: ["down2_2"], 9: ["down2_3"],
     10: ["stats1_1"], 11: ["ffn2", "attnT"], 12: ["kT", "kSplit", "aggr1"], 13: ["proj", "attnAdd", "store"],
     14: ["qT"], 15: ["qSplit", "xT1"]},
    {0: ["lo1"], 2: ["place", "stats3_0"], 3: ["gate1_0"], 5: ["silu1_0"], 7: ["up1_0", "stats3_1"],
     9: ["gate1_1", "aggr3"], 10: ["norm3"], 11: ["silu1_1", "res", "hid1_0"], 13: ["up1_1", "hid1_1"]},
    {0: ["xT3", "lo3"], 2: ["gate1_2"], 3: ["silu1_2", "up1_2"], 5: ["hid1_2", "norm1"], 7: ["down1_0"],
     9: ["down1_1"], 11: ["down1_2"], 13: ["down1_3", "ffn1"], 15: ["stats2_0"]},
]
AHEAD = {"load": 3, "stats1": 3, "aggr1": 3, "norm1": 3,
         "xT1": 2, "lo1": 2, "gate1": 2, "silu1": 2, "up1": 2, "hid1": 2, "down1": 2, "ffn1": 2, "stats2_0": 2,
         "stats2_1": 1, "aggr2": 1, "norm2": 1, "xT2": 1, "qkv": 1, "rope": 1, "kT": 1, "kSplit": 1, "qT": 1,
         "qSplit": 1, "place": 1, "res": 1,
         "attnT": -1, "proj": -1, "attnAdd": -1, "stats3": -1, "aggr3": -1, "norm3": -1, "xT3": -1, "lo3": -1,
         "gate2": -2, "silu2": -2, "up2": -2, "hid2": -2, "down2": -2, "ffn2": -2, "store": -2}
SLOT_AHEAD = {"maxT": 1, "maxRows": 1, "negHi": 1, "negLo": 1, "vAug": 1, "pv": -1, "oCopy": -1, "oT": -2, "oDiv": -2}


def ahead(what):
    return AHEAD.get(what, AHEAD.get(what.split("_")[0], 0))


def steps(b):
    out = []

    def exists(slot):
        return 0 <= slot < SLOTS

    for g in range(GROUPS):
        s = GROUPS * b + g
        for i in range(TILES):
            if exists(s):
                out.append(("exp", g, i))
            for what in BY_GROUP[g].get(i, []):
                if 0 <= b + ahead(what) < B:
                    out.append((what,))
            if exists(s + (i + LEAD) // TILES + 1):
                out.append(("max", g, i + LEAD))
            for what in EVERY_SLOT.get(i, []):
                if exists(s + SLOT_AHEAD[what.split("_")[0]]):
                    out.append((what, g))
    return out


ORDER = steps(B // 2)


DENSE_USERS = ("maxT", "oT", "xT1", "xT2", "xT3", "kT", "qT", "attnT", "proj", "down1_0", "down2_0",
               "qkv_0", "qkv_1", "qkv_2", "qkv_3") + tuple(
                   f"{k}{f}_{j}" for k in ("gate", "up") for f in (1, 2) for j in range(J))
SPLITS = ("xT1", "xT3", "kT", "qT")
BATCHES = range(-max(AHEAD.values()), B - min(AHEAD.values()))
FIRST, LAST = 3, 12


def number_uses():
    use, done, gate, stat, split = {}, {}, {}, {}, {}
    for b in BATCHES:
        for st in steps(b):
            for table, member in ((use, st[0] in DENSE_USERS), (gate, st[0].startswith("gate")),
                                  (stat, st[0].startswith("aggr")), (split, st[0] in SPLITS)):
                if member:
                    table[st, b] = len(table)
            if st[0] in DENSE_USERS and not st[0].startswith("down"):
                done[st, b] = len(done)
            elif st[0] in ("down1_3", "down2_3"):
                done[(st[0][:-1] + "0",), b] = len(done)
    return use, done, gate, stat, split


class Batch:

    def __init__(self, first, turn=None):
        self.first, self.turn = first, turn

    def value(self, per_batch, plus):
        v = per_batch * self.first + plus
        return v if self.turn is None else self.turn * (2 * per_batch) + v

    def counted(self, table, key, per=1, plus=0):
        v = table[key, self.first]
        if self.turn is None:
            return v // per + plus
        grow = table[key, self.first + 2] - v
        assert grow % per == 0 and grow == table[key, self.first + 4] - table[key, self.first + 2]
        return self.turn * (grow // per) + (v // per + plus)


def macaron_layer(nc, x, qkv_w, qkv_b, proj_w, proj_b, w_gate, w_up, w_down, rope_cos, rope_sin, out):
    USE, DONE, GATE, STAT, SPLIT = number_uses()
    with ExitStack() as ctx:
        def sb(name, shape, dt=F32):
            return ctx.enter_context(nc.sbuf_tensor(name, shape, dt))

        def ps(name):
            return ctx.enter_context(nc.psum_tensor(name, [P, L], F32))

        def sem(name):
            return ctx.enter_context(nc.semaphore(name))

        ident = sb("ident", [P, P])
        ones = sb("ones", [8, L], F32R)
        zeros = sb("zeros", [8, L], F32R)
        cos_t = sb("cos_t", [P, T, D])
        sin_t = sb("sin_t", [P, T, D])
        probs = [sb(f"probs{k}", [P, 4, T, L]) for k in range(2)]
        rows_int = probs[1][:, 0, :, :].rearrange("p t q -> p (t q)")[:, 0:3 * HID].bitcast(I32)
        rows_ffn = probs[1][:, 1, :, :].rearrange("p t q -> p (t q)")[:, 0:3 * HID]
        rows_qkv = probs[1][:, 2, 0, :]
        w_hi = {k: sb(f"w_{k}_hi", [P, HID], F32R) for k in ("gate", "up")}
        w_lo = {k: sb(f"w_{k}_lo", [P, HID], F32R) for k in ("gate", "up")}
        w_downT = sb("w_downT", [P, J, C])
        w_qkvT = sb("w_qkvT", [P, 3 * C])
        w_projT = sb("w_projT", [P, C])
        b_qkv = sb("b_qkv", [P, 3 * C])
        b_proj = sb("b_proj", [P, C])
        minus_half = sb("minus_half", [P, T])
        x_in = [sb(f"x_in{k}", [P, T, C]) for k in range(2)]
        x_ffn1 = sb("x_ffn1", [P, T, C])
        x_res = [sb(f"x_res{k}", [P, T, C]) for k in range(2)]
        x_attn = sb("x_attn", [P, T, C])
        y_out = sb("y_out", [P, T, C])
        stats = [sb(f"stats{k}", [P, T, 6]) for k in range(3)]
        mean_var = [sb(f"mean_var{k}", [P, T, 2]) for k in range(3)]
        var_eps = [sb(f"var_eps{k}", [P, T]) for k in range(3)]
        rstd = [sb(f"rstd{k}", [P, T]) for k in range(3)]
        x_hat = [sb(f"x_hat{k}", [P, T, C]) for k in range(3)]
        xT_hi = {n: sb(f"xT{n}_hi", [P, L], F32R) for n in (1, 3)}
        xT_lo = {n: sb(f"xT{n}_lo", [P, L], F32R) for n in (1, 3)}
        xT_2 = sb("xT_2", [P, L])
        tanh = sb("tanh", [P, J, L])
        silu = [sb(f"silu{k}", [P, L]) for k in range(2)]
        hid = sb("hid", [P, J, L])
        qkv = [sb(f"qkv{k}", [P, T, 3 * C]) for k in range(2)]
        rot_a = sb("rot_a", [P, T, 2 * C])
        rot_b = sb("rot_b", [P, T, 2 * C])
        hi = {k: sb(f"{k}_hi", [P, L], F32R) for k in "qk"}
        lo = {k: sb(f"{k}_lo", [P, L], F32R) for k in "qk"}
        operand = {k: [sb(f"{k}_op{n}", [P, GROUPS, L], F32R) for n in range(2)] for k in "qk"}
        v_aug = [sb(f"v_aug{k}", [P, T, 4, STRIP]) for k in range(2)]
        neg_max = [sb(f"neg_max{k}", [P, T, 4]) for k in range(2)]
        max_parts = [sb(f"max_parts{k}", [P, T, 8]) for k in range(2)]
        max_rows = [sb(f"max_rows{k}", [8, L], F32R) for k in range(2)]
        oT = sb("oT", [P, L])
        recip = [sb(f"recip{k}", [P, T, 4]) for k in range(2)]
        attn = [sb(f"attn{k}", [P, T, C]) for k in range(2)]
        attnT = sb("attnT", [P, L])
        max_ps = [ps(f"max_ps{k}") for k in range(2)]
        exp_ps = [ps(f"exp_ps{k}") for k in range(2)]
        pv_ps = ps("pv_ps")
        dense_ps = [ps(f"dense_ps{k}") for k in range(N_DENSE)]

        weights_in = sem("weights_in")
        tables_in = sem("tables_in")
        ident_zero = sem("ident_zero")
        ident_ready = sem("ident_ready")
        set_once = sem("set_once")
        ones_placed = sem("ones_placed")
        dequantized = sem("dequantized")
        setup_T = sem("setup_T")
        weights_ready = sem("weights_ready")
        weights_lo = sem("weights_lo")
        x_loaded = [sem(f"x_loaded{k}") for k in range(2)]
        stored = sem("stored")
        dense_ready = sem("dense_ready")
        dense_read = [sem(f"dense_read{k}") for k in range(N_DENSE)]
        tanh_ready = sem("tanh_ready")
        hi_ready = sem("hi_ready")
        stats_part = sem("stats_part")
        stats_ready = [sem(f"stats_ready{k}") for k in range(3)]
        var_ready = sem("var_ready")
        rstd_ready = [sem(f"rstd_ready{k}") for k in range(3)]
        hat_ready = [sem(f"hat_ready{k}") for k in range(3)]
        res_ready = sem("res_ready")
        rope_part = sem("rope_part")
        rot_ready = sem("rot_ready")
        bias_v = sem("bias_v")
        placed = [sem(f"placed{g}") for g in range(GROUPS)]
        v_ready = sem("v_ready")
        maxscore_ready = sem("maxscore_ready")
        max_done = sem("max_done")
        negmax_hi = sem("negmax_hi")
        negmax_ready = sem("negmax_ready")
        maxrows_placed = [sem(f"maxrows_placed{k}") for k in range(2)]
        expscore_ready = sem("expscore_ready")
        exp_done = sem("exp_done")
        pv_done = sem("pv_done")
        o_copied = sem("o_copied")
        recip_done = sem("recip_done")
        passed = sem("passed")

        SET_ONCE = 11
        PLACE_DMAS = 7

        def wait(eng, s, value):
            if not (isinstance(value, int) and value <= 0):
                eng.wait_ge(s, value)

        def settle(eng):
            eng.sem_inc(passed, 1)

        def wait_dense(eng, st, b):
            wait(eng, dense_ready, b.counted(DONE, st, plus=1))

        def bank(st, b):
            return USE[st, b.first] % N_DENSE

        def wait_read(eng, st, b):
            wait(eng, dense_read[bank(st, b)], b.counted(USE, st, per=N_DENSE, plus=1))

        def work(st, b):
            return Batch(b.first + ahead(st[0]), b.turn)

        def since(st, b, earlier):
            return b if ORDER.index(earlier) < ORDER.index(st) else Batch(b.first - 1, b.turn)

        def slot(b, g):
            return Batch(b.first + g // GROUPS, b.turn), g % GROUPS

        def max_tile(b, st):
            return *slot(b, st[1] + 1 + st[2] // TILES), st[2] % TILES

        def head_strip(hs):
            return slice(STRIP * hs, STRIP * (hs + 1))

        def tile(t):
            return slice(t * P, (t + 1) * P)

        def flat(t):
            return t[:].rearrange("p t c -> p (t c)")

        def program(run, eng, setup=None):
            for b in range(BATCHES[0], FIRST):
                for st in steps(b):
                    run(st, Batch(b))
                if b == BATCHES[0] and setup:
                    setup()
            with eng.Fori(0, (LAST - FIRST + 1) // 2) as turn:
                for b in (FIRST, FIRST + 1):
                    for st in steps(b):
                        run(st, Batch(b, turn))
            for b in range(LAST + 1, BATCHES[-1] + 1):
                for st in steps(b):
                    run(st, Batch(b))

        x_d = x.rearrange("b (p t) c -> b p t c", t=T)
        out_d = out.rearrange("b (p t) c -> b p t c", t=T)
        block = ctx.enter_context(nc.Block())

        @block.sync
        def _(sp):
            def move(dst, src):
                return sp.dma_start(dst.bitcast(F32), src.bitcast(F32))

            for b in range(2):
                sp.dma_start(x_in[b][:], x_d[b]).then_inc(x_loaded[b], 16)
            for dst, src in (
                (rows_int[:, 0:HID].rearrange("p (j c) -> p j c", j=J), w_gate.rearrange("(j p) c -> p j c", p=P)),
                (rows_int[:, HID:2 * HID].rearrange("p (j c) -> p j c", j=J), w_up.rearrange("(j p) c -> p j c", p=P)),
                (rows_int[:, 2 * HID:3 * HID], w_down),
                (rows_qkv[:, 0:3 * C].rearrange("p (j c) -> p j c", j=J), qkv_w.rearrange("(j p) c -> p j c", p=P)),
                (rows_qkv[:, 3 * C:4 * C], proj_w),
            ):
                sp.dma_start(dst, src).then_inc(weights_in, 16)
            sp.dma_start(b_qkv[:], qkv_b.unsqueeze(0).broadcast_to([P, 3 * C])).then_inc(tables_in, 16)
            sp.dma_start(b_proj[:], proj_b.unsqueeze(0).broadcast_to([P, C])).then_inc(tables_in, 16)
            sp.dma_start(cos_t[:], rope_cos.rearrange("(p t) d -> p t d", t=T)).then_inc(tables_in, 16)
            sp.dma_start(sin_t[:], rope_sin.rearrange("(p t) d -> p t d", t=T)).then_inc(tables_in, 16)
            sp.wait_ge(set_once, SET_ONCE)
            for n in range(2):
                move(operand["k"][n][MAX_ROW:P:16, :, :], ones[:].unsqueeze(1).broadcast_to([8, GROUPS, L])).then_inc(ones_placed, 16)

            def run(st, b):
                what = st[0]
                wb = work(st, b)
                if what == "load":
                    if wb.turn is None and wb.first < 2:
                        return
                    sp.wait_ge(hat_ready[1], wb.value(1, -1))
                    n = wb.first % 2
                    sp.dma_start(x_in[n][:], x_d[wb.value(1, 0)]).then_inc(x_loaded[n], 16)
                elif what == "store":
                    wait_read(sp, ("down2_0",), b)
                    sp.dma_start(out_d[wb.value(1, 0)], y_out[:]).then_inc(stored, 16)
                elif what == "place":
                    n = wb.first % 2
                    wait_read(sp, ("qT",), b)
                    for g in range(GROUPS):
                        for k, parts in (("q", (hi, hi, lo)), ("k", (hi, lo, hi))):
                            for part, src in enumerate(parts):
                                move(operand[k][n][part:P:PARTS, g, :], src[k][head_strip(g), :]).then_inc(placed[g], 16)
                        move(operand["q"][n][MAX_ROW:P:16, g, :], zeros[:]).then_inc(placed[g], 16)

            program(run, sp)
            sp.wait_ge(stored, 16 * B)

        @block.gpsimd
        def _(pool):
            nc.gpsimd.memset(ident[:], 0.0).then_inc(ident_zero, 1)
            pool.wait_ge(ident_zero, 1)
            nc.gpsimd.affine_select(out=ident[:], in_=ident[:], compare_op=ALU.not_equal, fill=1.0, base=0,
                                    pattern=[[-1, P]], channel_multiplier=1).then_inc(ident_ready, 1)
            nc.gpsimd.memset(minus_half[:], -0.5).then_inc(set_once, 1)
            pool.wait_ge(set_once, 1)

            def setup():
                nc.gpsimd.memset(ones[:].bitcast(F32), 1.0).then_inc(set_once, 1)
                nc.gpsimd.memset(zeros[:].bitcast(F32), 0.0).then_inc(set_once, 1)
                for n in range(2):
                    nc.gpsimd.memset(operand["k"][n][:].bitcast(F32), 0.0).then_inc(set_once, 1)
                    nc.gpsimd.memset(operand["q"][n][:].bitcast(F32), 0.0).then_inc(set_once, 1)
                    nc.gpsimd.memset(v_aug[n][:, :, :, D:D + 1], 1.0).then_inc(set_once, 1)
                    nc.gpsimd.memset(v_aug[n][:, :, :, D + 1:STRIP], 0.0).then_inc(set_once, 1)
                pool.wait_ge(set_once, SET_ONCE)
                pool.wait_ge(tables_in, 16 * 4)
                pool.wait_ge(dequantized, 2)

            def rope_steps(b, wb):
                done = [0]

                def link(ins):
                    done[0] += 1
                    ins.then_inc(rope_part, 1)

                def linked():
                    pool.wait_ge(rope_part, wb.value(4, done[0]))

                wait_read(pool, ("qkv_3",), b)
                buf = qkv[wb.first % 2]
                qk = buf[:, :, 0:2 * C]
                link(nc.gpsimd.tensor_tensor(qk, qk, b_qkv[:, 0:2 * C].unsqueeze(1).broadcast_to([P, T, 2 * C]), ALU.add))
                linked()
                src = qk.rearrange("p t (h d) -> p t h d", d=D)
                ra = rot_a[:].rearrange("p t (h d) -> p t h d", d=D)
                rb = rot_b[:].rearrange("p t (h d) -> p t h d", d=D)
                link(nc.gpsimd.tensor_tensor(ra, src, cos_t[:].unsqueeze(2).broadcast_to([P, T, 2 * H, D]), ALU.mult))
                for e in range(2):
                    link(nc.gpsimd.tensor_tensor(
                        rb[:, :, :, e::2], src[:, :, :, 1 - e::2],
                        sin_t[:, :, e::2].unsqueeze(2).broadcast_to([P, T, 2 * H, D // 2]), ALU.mult))
                linked()
                nc.gpsimd.tensor_tensor(rot_a[:], rot_a[:], rot_b[:], ALU.add).then_inc(rot_ready, 1)
                v = buf[:, :, 2 * C:3 * C]
                nc.gpsimd.tensor_tensor(v, v, b_qkv[:, 2 * C:3 * C].unsqueeze(1).broadcast_to([P, T, C]),
                                        ALU.add).then_inc(bias_v, 1)

            def run(st, b):
                what = st[0]
                wb = work(st, b)
                if what.startswith("aggr"):
                    n = int(what[-1]) - 1
                    pool.wait_ge(stats_ready[n], wb.value(1, 1))
                    settle(pool)
                    nc.gpsimd.tensor_scalar(var_eps[n][:], mean_var[n][:, :, 1], EPS, None, ALU.add).then_inc(var_ready, 1)
                    pool.wait_ge(var_ready, b.counted(STAT, st, plus=1))
                    nc.gpsimd.tensor_tensor(rstd[n][:], var_eps[n][:], minus_half[:], ALU.pow).then_inc(rstd_ready[n], 1)
                elif what.startswith("norm"):
                    n = int(what[-1]) - 1
                    src = (x_in[wb.first % 2], x_ffn1, x_attn)[n]
                    if wb.first >= 1:
                        wait_dense(pool, (f"xT{n + 1}",), since(st, b, (f"xT{n + 1}",)))
                    pool.wait_ge(rstd_ready[n], wb.value(1, 1))
                    settle(pool)
                    for t in range(T):
                        ins = nc.gpsimd.tensor_scalar(x_hat[n][:, t, :], src[:, t, :], mean_var[n][:, t, 0:1],
                                                      rstd[n][:, t:t + 1], ALU.subtract, ALU.mult)
                    ins.then_inc(hat_ready[n], 1)
                elif what == "res":
                    if wb.first >= 2:
                        wait_read(pool, ("proj",), since(st, b, ("proj",)))
                    nc.gpsimd.tensor_tensor(x_res[wb.first % 2][:], x_ffn1[:],
                                            b_proj[:].unsqueeze(1).broadcast_to([P, T, C]),
                                            ALU.add).then_inc(res_ready, 1)
                elif what == "rope":
                    rope_steps(b, wb)
                elif what == "vAug":
                    nb, ng = slot(b, st[1] + 1)
                    pool.wait_ge(bias_v, nb.value(1, 1))
                    wait(pool, pv_done, nb.value(GROUPS, ng - 1))
                    settle(pool)
                    v = qkv[nb.first % 2][:, :, 2 * C + 4 * D * ng:2 * C + 4 * D * (ng + 1)]
                    nc.gpsimd.tensor_copy(v_aug[ng % 2][:, :, :, 0:D],
                                          v.rearrange("p t (h d) -> p t h d", d=D)).then_inc(v_ready, 1)

            program(run, pool, setup)

        @block.scalar
        def _(act):
            def setup():
                act.wait_ge(setup_T, 4)
                nc.scalar.copy(w_hi["gate"][:], max_ps[0][:, 0:HID]).then_inc(weights_ready, 1)
                nc.scalar.copy(w_hi["up"][:], max_ps[1][:, 0:HID]).then_inc(weights_ready, 1)
                nc.scalar.mul(w_downT[:], exp_ps[0][:, 0:HID].rearrange("p (j c) -> p j c", j=J), 0.25).then_inc(weights_ready, 1)
                nc.scalar.mul(w_qkvT[:, 0:C], exp_ps[1][:, 0:C], Q_SCALE).then_inc(weights_ready, 1)
                nc.scalar.copy(w_qkvT[:, C:3 * C], exp_ps[1][:, C:3 * C]).then_inc(weights_ready, 1)
                nc.scalar.copy(w_projT[:], exp_ps[1][:, 3 * C:4 * C]).then_inc(weights_ready, 1)

            def take(dst, st, b):
                wait_dense(act, st, b)
                k = bank(st, b)
                nc.scalar.copy(dst, dense_ps[k][:]).then_inc(dense_read[k], 1)

            def run(st, b):
                what = st[0]
                wb = work(st, b)
                if what == "exp":
                    g, i = st[1:]
                    if i == 0:
                        wait(act, pv_done, b.value(GROUPS, g - 1))
                    wait(act, expscore_ready, b.value(GROUPS * TILES, TILES * g + i + 1))
                    nc.scalar.activation(probs[g % 2][:, i // T, i % T, :], exp_ps[i % 2][:], ACT.Exp).then_inc(exp_done, 1)
                elif what in SPLITS:
                    wait_dense(act, st, b)
                    if what in ("kT", "qT"):
                        wait(act, placed[GROUPS - 1], wb.value(16 * PLACE_DMAS, 0))
                    dst = xT_hi[int(what[-1])] if what[0] == "x" else hi[what[0]]
                    nc.scalar.copy(dst[:], dense_ps[bank(st, b)][:]).then_inc(hi_ready, 1)
                elif what == "xT2":
                    take(xT_2[:], st, b)
                elif what == "attnT":
                    take(attnT[:], st, b)
                elif what.startswith("qkv"):
                    wait_dense(act, st, b)
                    k = bank(st, b)
                    nc.scalar.copy(qkv[wb.first % 2][:, int(what[-1]), :], dense_ps[k][:, 0:3 * C]).then_inc(dense_read[k], 1)
                elif what == "maxT":
                    nb, ng = slot(b, st[1] + 1)
                    wait_dense(act, st, b)
                    wait(act, maxrows_placed[ng % 2], nb.value(32, 16 * (ng // 2)))
                    k = bank(st, b)
                    nc.scalar.copy(max_rows[ng % 2][:], dense_ps[k][0:8, :]).then_inc(dense_read[k], 1)
                elif what == "maxRows":
                    nb, ng = slot(b, st[1] + 1)
                    wait_read(act, ("maxT", st[1]), b)
                    act.dma_start(operand["q"][nb.first % 2][MAX_ROW:P:16, ng, :].bitcast(F32),
                                  max_rows[ng % 2][:].bitcast(F32)).then_inc(maxrows_placed[ng % 2], 16)
                elif what == "oCopy":
                    pb, pg = slot(b, st[1] - 1)
                    wait(act, pv_done, pb.value(GROUPS, pg + 1))
                    if (("oT", st[1]), b.first) in USE:
                        wait_dense(act, ("oT", st[1]), b)
                    nc.scalar.copy(oT[:], pv_ps[:]).then_inc(o_copied, 1)
                elif what.startswith("gate"):
                    wait_dense(act, st, b)
                    n, j = int(what[4]) - 1, int(what[-1])
                    if b.turn is not None:
                        last = (f"gate{2 - n}_{j}",)
                        wait_read(act, last, since(st, b, last))
                    elif GATE[st, b.first] >= J:
                        (last, lb), = [key for key, at in GATE.items() if at == GATE[st, b.first] - J]
                        wait_read(act, last, Batch(lb))
                    nc.scalar.activation(tanh[:, j, :], dense_ps[bank(st, b)][:], ACT.Tanh, scale=0.5).then_inc(tanh_ready, 1)

            program(run, act, setup)

        @block.vector
        def _(dve):
            dve.wait_ge(weights_in, 16 * 5)
            nc.vector.tensor_scalar(rows_ffn, rows_int, W_SCALE, None,
                                    ALU.mult).then_inc(dequantized, 1)
            dve.wait_ge(tables_in, 16 * 4)
            nc.vector.tensor_scalar(b_qkv[:, 0:C], b_qkv[:, 0:C], Q_SCALE, None, ALU.mult).then_inc(dequantized, 1)

            def setup():
                dve.wait_ge(weights_ready, 2)
                for k, bank_of in (("gate", max_ps[0]), ("up", max_ps[1])):
                    nc.vector.tensor_tensor(w_lo[k][:], bank_of[:, 0:HID], w_hi[k][:].bitcast(F32),
                                            ALU.subtract).then_inc(weights_lo, 1)

            def split_lo(dst, high, st, b):
                wait(dve, hi_ready, b.counted(SPLIT, st, plus=1))
                k = bank(st, b)
                nc.vector.tensor_tensor(dst[:], dense_ps[k][:], high[:].bitcast(F32), ALU.subtract).then_inc(dense_read[k], 1)

            def run(st, b):
                what = st[0]
                wb = work(st, b)
                k = bank(st, b) if what in DENSE_USERS else None
                if what == "max":
                    nb, ng, v = max_tile(b, st)
                    wait(dve, maxscore_ready, nb.value(GROUPS * TILES, TILES * ng + v + 1))
                    nc.vector.tensor_reduce(neg_max[ng % 2][:, v % T, v // T:v // T + 1], max_ps[v % 2][:],
                                            AX_X, ALU.max, negate=True).then_inc(max_done, 1)
                elif what in ("negHi", "negLo"):
                    nb, ng = slot(b, st[1] + 1)
                    m = neg_max[ng % 2][:]
                    parts = max_parts[ng % 2][:].rearrange("p t (h x) -> p t h x", x=2)
                    if what == "negHi":
                        wait(dve, max_done, nb.value(GROUPS * TILES, TILES * (ng + 1)))
                        nc.vector.tensor_copy(parts[:, :, :, 0].bitcast(F32R), m).then_inc(negmax_hi, 1)
                    else:
                        wait(dve, negmax_hi, nb.value(GROUPS, ng + 1))
                        nc.vector.tensor_tensor(parts[:, :, :, 1].bitcast(F32R), m, parts[:, :, :, 0],
                                                ALU.subtract).then_inc(negmax_ready, 1)
                elif what == "oDiv":
                    pb, pg = slot(b, st[1] - 2)
                    st = ("oT", st[1])
                    k = bank(st, b)
                    o = dense_ps[k][:].rearrange("p (t h r) -> p t h r", t=T, r=STRIP)
                    wait_dense(dve, st, b)
                    nc.vector.reciprocal(recip[pg % 2][:], o[:, :, :, D]).then_inc(recip_done, 1)
                    wait(dve, recip_done, pb.value(GROUPS, pg + 1))
                    a = attn[pb.first % 2][:, :, 4 * D * pg:4 * D * (pg + 1)].rearrange("p t (h d) -> p t h d", d=D)
                    nc.vector.tensor_tensor(a, o[:, :, :, 0:D], recip[pg % 2][:].unsqueeze(3).broadcast_to([P, T, 4, D]),
                                            ALU.mult).then_inc(dense_read[k], 1)
                elif what in ("lo1", "lo3"):
                    n = int(what[-1])
                    split_lo(xT_lo[n], xT_hi[n], (f"xT{n}",), since(st, b, (f"xT{n}",)))
                elif what in ("kSplit", "qSplit"):
                    split_lo(lo[what[0]], hi[what[0]], (f"{what[0]}T",), b)
                elif what.startswith("silu"):
                    g_st = (what.replace("silu", "gate"),)
                    n, k = GATE[g_st, b.first], bank(g_st, b)
                    wait(dve, tanh_ready, b.counted(GATE, g_st, plus=1))
                    nc.vector.scalar_tensor_tensor(silu[n % 2][:], tanh[:, int(what[-1]), :], 1.0,
                                                   dense_ps[k][:], ALU.add, ALU.mult).then_inc(dense_read[k], 1)
                elif what.startswith("hid"):
                    g_st, u_st = (what.replace("hid", "gate"),), (what.replace("hid", "up"),)
                    n, k = GATE[g_st, b.first], bank(u_st, b)
                    wait_dense(dve, u_st, b)
                    wait_read(dve, g_st, b)
                    nc.vector.tensor_tensor(hid[:, int(what[-1]), :], silu[n % 2][:], dense_ps[k][:],
                                            ALU.mult).then_inc(dense_read[k], 1)
                elif what.startswith("stats"):
                    n, half = int(what[5]) - 1, int(what[-1])
                    src = (x_in[wb.first % 2], x_ffn1, x_attn)[n]
                    if not half:
                        wait(dve, stats_ready[n], wb.value(1, 0))
                        if n == 0:
                            wait(dve, x_loaded[wb.first % 2], wb.value(8, 16 if wb.first % 2 == 0 else 8))
                        else:
                            wait_read(dve, (("down1_0",), ("proj",))[n - 1], b)
                    for t in (2 * half, 2 * half + 1):
                        nc.vector.bn_stats(stats[n][:, t, :], src[:, t, :]).then_inc(stats_part, 1)
                elif what.startswith("aggr"):
                    n = int(what[-1]) - 1
                    wait(dve, hat_ready[n], wb.value(1, 0))
                    dve.wait_ge(stats_part, b.counted(STAT, st, plus=1) * T)
                    settle(dve)
                    for t in range(T):
                        ins = nc.vector.bn_aggr(mean_var[n][:, t, :], stats[n][:, t, :])
                    ins.then_inc(stats_ready[n], 1)
                elif what == "ffn1":
                    st = ("down1_0",)
                    k = bank(st, b)
                    wait_dense(dve, st, b)
                    wait(dve, res_ready, wb.value(1, 0))
                    nc.vector.tensor_tensor(flat(x_ffn1), dense_ps[k][:], flat(x_in[wb.first % 2]), ALU.add).then_inc(dense_read[k], 1)
                elif what == "attnAdd":
                    st = ("proj",)
                    k = bank(st, b)
                    wait_dense(dve, st, b)
                    if wb.first >= 1:
                        wait_read(dve, ("down2_0",), since(st, b, ("down2_0",)))
                    wait(dve, res_ready, wb.value(1, 1))
                    nc.vector.tensor_tensor(flat(x_attn), dense_ps[k][:], flat(x_res[wb.first % 2]), ALU.add).then_inc(dense_read[k], 1)
                elif what == "ffn2":
                    st = ("down2_0",)
                    k = bank(st, b)
                    wait_dense(dve, st, b)
                    wait(dve, stored, wb.value(16, 0))
                    nc.vector.tensor_tensor(flat(y_out), dense_ps[k][:], flat(x_attn), ALU.add).then_inc(dense_read[k], 1)

            program(run, dve, setup)

        @block.tensor
        def _(pe):
            pe.wait_ge(ident_ready, 1)
            pe.wait_ge(dequantized, 2)
            pe.wait_ge(weights_in, 16 * 5)
            for n, dst, src in ((J, max_ps[0], rows_ffn[:, 0:HID]), (J, max_ps[1], rows_ffn[:, HID:2 * HID]),
                                (J, exp_ps[0], rows_ffn[:, 2 * HID:3 * HID]), (4, exp_ps[1], rows_qkv)):
                for j in range(n):
                    ins = nc.tensor.transpose(dst[:, tile(j)], src[:, tile(j)], ident[:])
                ins.then_inc(setup_T, 1)
            pe.wait_ge(weights_ready, 6)
            pe.wait_ge(weights_lo, 2)

            def transposes(st, b, src):
                k = bank(st, b)
                for t in range(T):
                    ins = nc.tensor.transpose(dense_ps[k][:, tile(t)], src(t), ident[:])
                ins.then_inc(dense_ready, 1)

            def run(st, b):
                what = st[0]
                wb = work(st, b)
                if what in DENSE_USERS:
                    k = bank(st, b)
                    wait(pe, dense_read[k], b.counted(USE, st, per=N_DENSE))
                if what == "exp":
                    g, i = st[1:]
                    hs, t = divmod(i, T)
                    if i == 0:
                        pe.wait_ge(maxrows_placed[g % 2], b.value(32, 16 * (g // 2) + 16))
                    wait(pe, exp_done, b.value(GROUPS * TILES, TILES * g + i - 1))
                    n = b.first % 2
                    nc.tensor.matmul(exp_ps[i % 2][:], operand["k"][n][head_strip(hs), g, tile(t)],
                                     operand["q"][n][head_strip(hs), g, :],
                                     start=True, stop=True).then_inc(expscore_ready, 1)
                elif what == "max":
                    nb, ng, v = max_tile(b, st)
                    hs, t = divmod(v, T)
                    if (nb.first, nb.turn, ng, v) == (0, None, 0, 0):
                        pe.wait_ge(ones_placed, 16 * 2)
                    if v == 0:
                        pe.wait_ge(placed[ng], nb.value(16 * PLACE_DMAS, 16 * PLACE_DMAS))
                    wait(pe, max_done, nb.value(GROUPS * TILES, TILES * ng + v - 1))
                    n = nb.first % 2
                    nc.tensor.matmul(max_ps[v % 2][:], operand["q"][n][head_strip(hs), ng, tile(t)],
                                     operand["k"][n][head_strip(hs), ng, :],
                                     start=True, stop=True).then_inc(maxscore_ready, 1)
                elif what == "maxT":
                    nb, ng = slot(b, st[1] + 1)
                    wait(pe, negmax_ready, nb.value(GROUPS, ng + 1))
                    for t in range(T):
                        ins = nc.tensor.transpose(dense_ps[k][0:8, tile(t)], max_parts[ng % 2][:, t, :], ident[:])
                    ins.then_inc(dense_ready, 1)
                elif what.startswith("pv"):
                    pb, pg = slot(b, st[1] - 1)
                    t = int(what[-1])
                    if t == 0:
                        wait(pe, exp_done, pb.value(GROUPS * TILES, TILES * (pg + 1)))
                        wait(pe, v_ready, pb.value(GROUPS, pg + 1))
                        wait(pe, o_copied, pb.value(GROUPS, pg))
                    for hs in range(4):
                        ins = nc.tensor.matmul(pv_ps[head_strip(hs), :], v_aug[pg % 2][:, t, hs, :],
                                               probs[pg % 2][:, hs, t, :], start=(t == 0), stop=(t == T - 1))
                    if t == T - 1:
                        ins.then_inc(pv_done, 1)
                elif what == "oT":
                    pb, pg = slot(b, st[1] - 2)
                    wait(pe, o_copied, pb.value(GROUPS, pg + 1))
                    transposes(st, b, lambda t: oT[:, tile(t)])
                elif what in ("kT", "qT"):
                    pe.wait_ge(rot_ready, wb.value(1, 1))
                    at = 0 if what == "qT" else C
                    transposes(st, b, lambda t: rot_a[:, t, at:at + C])
                elif what in ("xT1", "xT2", "xT3"):
                    n = int(what[-1]) - 1
                    pe.wait_ge(hat_ready[n], wb.value(1, 1))
                    transposes(st, b, lambda t: x_hat[n][:, t, :])
                elif what.startswith(("gate", "up")):
                    n, j = {"1": 1, "2": 3}[what[-3]], int(what[-1])
                    w = what[:-3]
                    if j == 0 and w == "gate":
                        wait_read(pe, (f"xT{n}",), since(st, b, (f"xT{n}",)))
                    for m, (a, c) in enumerate(((w_hi, xT_hi), (w_hi, xT_lo), (w_lo, xT_hi))):
                        ins = nc.tensor.matmul(dense_ps[k][:], a[w][:, tile(j)], c[n][:], start=(m == 0), stop=(m == 2))
                    ins.then_inc(dense_ready, 1)
                elif what.startswith("down"):
                    t = int(what[-1])
                    first = (what[:-1] + "0",)
                    k = bank(first, b)
                    if t == 0:
                        up = (f"up{what[4]}_{J - 1}",)
                        wait_read(pe, up, since(st, b, up))
                    for j in range(J):
                        ins = nc.tensor.matmul(dense_ps[k][:, tile(t)], hid[:, j, tile(t)], w_downT[:, j, :],
                                               start=(j == 0), stop=(j == J - 1))
                    if t == T - 1:
                        ins.then_inc(dense_ready, 1)
                elif what.startswith("qkv"):
                    if what == "qkv_0":
                        wait_read(pe, ("xT2",), b)
                    nc.tensor.matmul(dense_ps[k][:, 0:3 * C], xT_2[:, tile(int(what[-1]))], w_qkvT[:],
                                     start=True, stop=True).then_inc(dense_ready, 1)
                elif what == "attnT":
                    wait_read(pe, ("oT", 1), b)
                    transposes(st, b, lambda t: attn[wb.first % 2][:, t, :])
                elif what == "proj":
                    wait_read(pe, ("attnT",), b)
                    for t in range(T):
                        ins = nc.tensor.matmul(dense_ps[k][:, tile(t)], attnT[:, tile(t)], w_projT[:],
                                               start=True, stop=True)
                    ins.then_inc(dense_ready, 1)

            program(run, pe)


_INS = ["L0_attn_x", "L0_attn_qkv_w", "L0_attn_qkv_b", "L0_attn_proj_w", "L0_attn_proj_b",
        "L0_ffn_w_gate", "L0_ffn_w_up", "L0_ffn_w_down"]


def rope_tables():
    import numpy as np

    inv_freq = (np.float32(1.0) / np.float32(10000.0) ** (np.arange(0, D, 2, dtype=np.float32) / np.float32(D))).astype(np.float32)
    freqs = np.arange(L, dtype=np.float32)[:, None] * inv_freq[None, :]
    angle = np.concatenate([freqs, freqs], axis=-1).astype(np.float64)
    sign = np.where(np.arange(D) % 2 == 0, -1.0, 1.0)
    return np.cos(angle).astype(np.float32), (np.sin(angle) * sign).astype(np.float32)


def kernel(**inputs):
    import numpy as np
    import concourse.bacc as bacc
    from concourse.bass_utils import run_bass_kernel_spmd

    nc = bacc.Bacc("TRN2", target_bir_lowering=False, num_devices=1)
    arrays = {name: np.ascontiguousarray(inputs[name]) for name in _INS}
    arrays["rope_cos"], arrays["rope_sin"] = rope_tables()
    args = [nc.dram_tensor(name, a.shape, mybir.dt.from_np(a.dtype), kind="ExternalInput").ap()
            for name, a in arrays.items()]
    out = nc.dram_tensor("out", (B, L, C), F32, kind="ExternalOutput").ap()
    macaron_layer(nc, *args, out)
    result = run_bass_kernel_spmd(nc, [arrays], core_ids=[0])
    return result.results[0]["out"]
```
